# Optimizing a Trainium2 kernel written in Bass

```python
import numpy as np
import jax
import jax.numpy as jnp

def _softmax(x, axis=-1):
    return jax.nn.softmax(x, axis=axis)

def _gelu(x):
    return jax.nn.gelu(x, approximate=True)

def _silu(x):
    return jax.nn.silu(x)

def _sigmoid(x):
    return jax.nn.sigmoid(x)

def _layernorm(x, axis=-1, eps=1e-05):
    m = jnp.mean(x, axis=axis, keepdims=True)
    v = jnp.var(x, axis=axis, keepdims=True)
    return (x - m) / jnp.sqrt(v + eps)

def _scatter_add(tgt, idx, src, axis=0):
    return tgt.at[idx].add(src)

def _segment_sum(src, seg, n):
    return jax.ops.segment_sum(src, seg, n)
kernel_name = 'mk_sandwich_d1_jaxref_r4_a15259'

def setup_inputs(seed: int=0):
    np.random.seed(seed)
    _w = jnp.asarray

    def _L0_attn_setup():
        import jax, jax.numpy as jnp
        import numpy as np
        D_MODEL = 256
        NHEAD = 16
        HEAD_DIM = D_MODEL // NHEAD

        def _rope(x, sin, cos):
            half = x.shape[-1] // 2
            x1, x2 = (x[..., :half], x[..., half:])
            rotated = jnp.concatenate([-x2, x1], axis=-1)
            return x * cos + rotated * sin
        key = jax.random.key(seed)
        ks = jax.random.split(key, 9)
        s = 0.02
        x = jax.random.normal(ks[0], (2, 512, D_MODEL), dtype=jnp.float32)
        Wq = jax.random.normal(ks[1], (D_MODEL, D_MODEL), dtype=jnp.float32) * s
        bq = jnp.zeros((D_MODEL,), jnp.float32)
        Wk = jax.random.normal(ks[2], (D_MODEL, D_MODEL), dtype=jnp.float32) * s
        bk = jnp.zeros((D_MODEL,), jnp.float32)
        Wv = jax.random.normal(ks[3], (D_MODEL, D_MODEL), dtype=jnp.float32) * s
        bv = jnp.zeros((D_MODEL,), jnp.float32)
        Wo = jax.random.normal(ks[4], (D_MODEL, D_MODEL), dtype=jnp.float32) * s
        bo = jnp.zeros((D_MODEL,), jnp.float32)
        return {'x': x, 'Wq': Wq, 'bq': bq, 'Wk': Wk, 'bk': bk, 'Wv': Wv, 'bv': bv, 'Wo': Wo, 'bo': bo}
    _L0_attn_in = _L0_attn_setup()

    def _L0_ffn_setup():
        import jax, jax.numpy as jnp
        import numpy as np
        D_MODEL = 256
        H_SHARED = 512
        H_ROUTED = 256
        N_EXPERTS = 8
        TOP_K = 2
        key = jax.random.key(seed)
        ks = jax.random.split(key, 8)
        B, T = (2, 512)
        sc_d = 1.0 / np.sqrt(D_MODEL)
        sc_hs = 1.0 / np.sqrt(H_SHARED)
        sc_hr = 1.0 / np.sqrt(H_ROUTED)
        return {'x': jax.random.normal(ks[0], (B, T, D_MODEL), dtype=jnp.float32), 'router_w': jax.random.normal(ks[1], (N_EXPERTS, D_MODEL), dtype=jnp.float32) * sc_d, 'router_bias': jnp.zeros((N_EXPERTS,), dtype=jnp.float32), 'sw1': jax.random.normal(ks[2], (D_MODEL, H_SHARED), dtype=jnp.float32) * sc_d, 'sw3': jax.random.normal(ks[3], (D_MODEL, H_SHARED), dtype=jnp.float32) * sc_d, 'sw2': jax.random.normal(ks[4], (H_SHARED, D_MODEL), dtype=jnp.float32) * sc_hs, 'ew1': jax.random.normal(ks[5], (N_EXPERTS, D_MODEL, H_ROUTED), dtype=jnp.float32) * sc_d, 'ew2': jax.random.normal(ks[6], (N_EXPERTS, H_ROUTED, D_MODEL), dtype=jnp.float32) * sc_hr}
    _L0_ffn_in = _L0_ffn_setup()
    _d = {'L0_attn_x': _L0_attn_in['x'], 'L0_attn_Wq': _L0_attn_in['Wq'], 'L0_attn_bq': _L0_attn_in['bq'], 'L0_attn_Wk': _L0_attn_in['Wk'], 'L0_attn_bk': _L0_attn_in['bk'], 'L0_attn_Wv': _L0_attn_in['Wv'], 'L0_attn_bv': _L0_attn_in['bv'], 'L0_attn_Wo': _L0_attn_in['Wo'], 'L0_attn_bo': _L0_attn_in['bo'], 'L0_ffn_router_w': _L0_ffn_in['router_w'], 'L0_ffn_router_bias': _L0_ffn_in['router_bias'], 'L0_ffn_sw1': _L0_ffn_in['sw1'], 'L0_ffn_sw3': _L0_ffn_in['sw3'], 'L0_ffn_sw2': _L0_ffn_in['sw2'], 'L0_ffn_ew1': _L0_ffn_in['ew1'], 'L0_ffn_ew2': _L0_ffn_in['ew2']}
    _x0 = _d['L0_attn_x']
    _d['L0_attn_x'] = jax.random.normal(jax.random.fold_in(jax.random.key(seed), 1), (32, 512, 256), dtype=_x0.dtype)
    del _x0
    return _d

def reference(L0_attn_x, L0_attn_Wq, L0_attn_bq, L0_attn_Wk, L0_attn_bk, L0_attn_Wv, L0_attn_bv, L0_attn_Wo, L0_attn_bo, L0_ffn_router_w, L0_ffn_router_bias, L0_ffn_sw1, L0_ffn_sw3, L0_ffn_sw2, L0_ffn_ew1, L0_ffn_ew2):

    def _L0_attn_ref(x, Wq, bq, Wk, bk, Wv, bv, Wo, bo):
        import jax, jax.numpy as jnp
        import numpy as np
        D_MODEL = 256
        NHEAD = 16
        HEAD_DIM = D_MODEL // NHEAD

        def _rope(x, sin, cos):
            half = x.shape[-1] // 2
            x1, x2 = (x[..., :half], x[..., half:])
            rotated = jnp.concatenate([-x2, x1], axis=-1)
            return x * cos + rotated * sin
        B, L, D = x.shape
        H, Dh = (NHEAD, HEAD_DIM)
        q = (x @ Wq.T + bq).reshape(B, L, H, Dh)
        k = (x @ Wk.T + bk).reshape(B, L, H, Dh)
        v = (x @ Wv.T + bv).reshape(B, L, H, Dh)
        inv_freq = 1.0 / 10000.0 ** (jnp.arange(0, Dh, 2, dtype=jnp.float32) / Dh)
        t = jnp.arange(L, dtype=jnp.float32)
        freqs = jnp.einsum('i,j->ij', t, inv_freq)
        emb = jnp.concatenate([freqs, freqs], axis=-1)
        cos = jnp.cos(emb)[None, :, None, :]
        sin = jnp.sin(emb)[None, :, None, :]
        q = _rope(q, sin, cos)
        k = _rope(k, sin, cos)
        scores = jnp.einsum('bqhd,bkhd->bhqk', q, k) / jnp.sqrt(jnp.float32(Dh))
        attn = jax.nn.softmax(scores, axis=-1)
        out = jnp.einsum('bhqk,bkhd->bqhd', attn, v).reshape(B, L, D)
        return out @ Wo.T + bo

    def _L0_ffn_ref(x, router_w, router_bias, sw1, sw3, sw2, ew1, ew2):
        import jax, jax.numpy as jnp
        import numpy as np
        D_MODEL = 256
        H_SHARED = 512
        H_ROUTED = 256
        N_EXPERTS = 8
        TOP_K = 2
        B, T, C = x.shape
        xf = x.reshape(-1, C)
        shared_out = jax.nn.silu(xf @ sw1) * (xf @ sw3) @ sw2
        s = jax.nn.sigmoid((xf @ router_w.T).astype(jnp.float32))
        sel_scores = s + router_bias.astype(jnp.float32)
        _, topk_idx = jax.lax.top_k(sel_scores, TOP_K)
        s_sel = jnp.take_along_axis(s, topk_idx, axis=1)
        denom = s_sel.sum(axis=1, keepdims=True)
        gates = jnp.where(denom > 1e-09, s_sel / (denom + 1e-09), 1.0 / TOP_K).astype(x.dtype)
        one_hot = jax.nn.one_hot(topk_idx, N_EXPERTS, dtype=x.dtype)
        comb = jnp.einsum('nke,nk->ne', one_hot, gates)
        h = jax.nn.gelu(jnp.einsum('nd,edh->neh', xf, ew1), approximate=False)
        y = jnp.einsum('neh,ehd->ned', h, ew2)
        routed_out = jnp.einsum('ned,ne->nd', y, comb)
        return (shared_out + routed_out).reshape(B, T, C)
    x = L0_attn_x
    x = x + _layernorm(_L0_attn_ref(_layernorm(x, axis=-1), L0_attn_Wq, L0_attn_bq, L0_attn_Wk, L0_attn_bk, L0_attn_Wv, L0_attn_bv, L0_attn_Wo, L0_attn_bo), axis=-1)
    x = x + _layernorm(_L0_ffn_ref(_layernorm(x, axis=-1), L0_ffn_router_w, L0_ffn_router_bias, L0_ffn_sw1, L0_ffn_sw3, L0_ffn_sw2, L0_ffn_ew1, L0_ffn_ew2), axis=-1)
    return x

_drawn_inputs = setup_inputs


def setup_inputs(seed=0):
    import zlib

    import numpy as np

    out = dict(_drawn_inputs(seed))
    spreads = {'L0_attn_bq': (0.0, 0.7),
     'L0_attn_bk': (0.0, 0.8),
     'L0_attn_bv': (0.0, 0.1),
     'L0_attn_bo': (0.0, 0.1),
     'L0_ffn_router_bias': (0.0, 0.1)}
    factors = {'L0_attn_Wq': 3.175, 'L0_attn_Wk': 3.162}
    for name, (base, spread) in spreads.items():
        noise = np.random.default_rng([zlib.crc32(name.encode()), seed]).standard_normal(out[name].shape)
        drawn = base * np.exp(spread * noise) if base else spread * noise
        out[name] = jnp.asarray(drawn.astype(out[name].dtype))
    for name, factor in factors.items():
        out[name] = (out[name] * factor).astype(out[name].dtype)
    return out
```

```python
import concourse.bass as bass
from concourse import mybir
from contextlib import ExitStack

F32 = mybir.dt.float32
F16 = mybir.dt.float16
U32 = mybir.dt.uint32
ACT = mybir.ActivationFunctionType
ALU = mybir.AluOpType
AX = mybir.AxisListType

NB, L, D = 32, 512, 256
H, DH = 16, 16
HS, HR, NE = 512, 256, 8
P = 128
NT = L // P
KT = D // P
MS = HS // P
MR = HR // P
EPS = 1e-5
WS = 64.0
SM = float(DH) ** -0.5

QK0 = 0
WV0 = QK0 + KT * 4 * D
WO0 = WV0 + KT * D
SA0 = WO0 + KT * D
SB0 = SA0 + KT * HS
SD0 = SB0 + KT * HS
EU0 = SD0 + MS * D
ED0 = EU0 + NE * KT * HR
RW0 = ED0 + NE * MR * D
WCOLS = RW0 + KT * NE
NCH = 8
CH = WCOLS // NCH
assert CH * NCH == WCOLS and CH <= 4 * L

NS = H * 2
NQ = 16
KR = 66

FIRST_HALF = (
    ["OT3", "V0", "V1", "DS0", "AT0", "AT1", "DS1", "D0", "WO0", "WO1", "LNO1", "D1", "D2", "LNO2", "D3", "LNC1",
     "D4", "D5", "LNC2", "D6", "XT0", "XT1"]
    + [f"D{n}" for n in range(7, 16)] + ["LNF1", "U0", "U1", "LNF2"] + [f"U{n}" for n in range(2, 16)]
    + [f"S{n}" for n in range(2 * MS)] + ["LNA1", "MT", "LNA2"]
)
BETWEEN = {1: ["XA0"], 2: ["XA1"], 3: ["RT"], 4: ["Q0"], 5: ["Q1", "GATE"], 6: ["OT0", "Q2"], 7: ["Q3"], 8: ["Q4"],
           9: ["Q5"], 10: ["OT1", "Q6"], 11: ["Q7"], 14: ["OT2"]}
SCORES_OVER = 42


def stage_of(item):
    if item[:2] in ("OT",):
        return "c" if item == "OT3" else "b"
    if item[0] == "V" or item == "MT":
        return "b"
    if item[0] == "D" or item[:3] == "LNF":
        return "d"
    if item[:2] == "XA" or item[0] == "Q" or item[:3] == "LNA":
        return "a"
    return "c"


SHIFT = {"a": 1, "b": 0, "c": -1, "d": -2}
USES_BANK = ("OT", "V", "DS", "AT", "D", "WO", "XT", "U", "S", "MT", "XA", "RT", "Q")


def uses_bank(item):
    return not item.startswith("LN") and item != "GATE"


def first_half():
    done = 0
    for n, item in enumerate(FIRST_HALF):
        upto = min(NS, (n + 1) * NS // SCORES_OVER)
        yield range(done, upto), item
        done = upto


class Step:

    def __init__(self, i, at, base, per):
        self.i, self.at, self.base, self.per = i, at, base, per
        self.has = {s: 0 <= at + SHIFT[s] < NB for s in SHIFT}
        self.plan, self.used = {}, [0, 0, 0]
        order = [x for _, x in first_half()] + [x for n in range(NQ) for x in BETWEEN.get(n, [])]
        n = 0
        for item in order:
            if uses_bank(item) and self.has[stage_of(item)]:
                self.plan[item] = (n % 3, self.used[n % 3])
                self.used[n % 3] += 1
                n += 1

    def count(self, stage, per, c):
        return self.i * per + (SHIFT[stage] * per + c)

    def first(self, stage):
        return self.at + SHIFT[stage] == 0

    def bank(self, item):
        return self.plan[item][0]

    def nth(self, item):
        bank, nth = self.plan[item]
        n = self.base[bank] + nth + 1
        return n if self.per is None else self.i * self.per[bank] + (n - self.at * self.per[bank])

    def refills(self, item):
        return self.base[self.plan[item][0]] + self.plan[item][1] > 0


def steps():
    base, out = [0, 0, 0], []
    for at in range(-1, NB + 2):
        s = Step(at, at, list(base), None)
        out.append(s)
        base = [b + u for b, u in zip(base, s.used)]
    return out


LOOP = (2, NB - 2)


def walk(eng, body):
    every = steps()
    for s in every:
        if s.at < LOOP[0] or s.at > LOOP[1]:
            body(s)
        elif s.at == LOOP[0]:
            with eng.Fori(LOOP[0], LOOP[1] + 1) as i:
                body(Step(i, s.at, s.base, list(s.used)))


def block_program(nc, x, wall, bqk, rows, tabs, iota, ident, zeros, out):
    ctx = ExitStack()
    with ctx:
        def sb(name, shape, dt):
            return ctx.enter_context(nc.sbuf_tensor(name, shape, dt))

        def sem(name):
            return ctx.enter_context(nc.semaphore(name))

        w_hi = sb("w_hi", [P, WCOLS], F16)
        w_lo = sb("w_lo", [P, WCOLS], F16)
        ident32 = sb("ident32", [P, P], F32)
        ident16 = sb("ident16", [P, P], F16)
        bqk_sb = sb("bqk_sb", [P, 8], F32)
        rows_sb = sb("rows_sb", [P, 2 * D + NE], F32)
        tabs_sb = sb("tabs_sb", [P, 2, L], F32)
        iota_sb = sb("iota_sb", [P, NE], F32)
        minus_half = sb("minus_half", [P, NT], F32)
        bv_b, bo_b, rb_b = rows_sb[:, 0:D], rows_sb[:, D:2 * D], rows_sb[:, 2 * D:]

        xin = sb("xin", [P, NT, D], F32)
        xnT_h = sb("xnT_h", [P, KT, L], F16)
        xnT_l = sb("xnT_l", [P, KT, L], F16)
        rope = sb("rope", [P, 2, L], F32)
        hid = rope
        rot_h = sb("rot_h", [P, 2, 2, L], F16)
        rot_l = sb("rot_l", [P, 2, 2, L], F16)
        qS = sb("qS", [P, H, L], F16)
        kS = sb("kS", [P, H, L], F16)
        vaug = sb("vaug", [P, NT, H, 32], F32)
        negm = sb("negm", [P, NT, H], F32)
        mcols = sb("mcols", [P, NT, 2 * H], F16)
        mrows = sb("mrows", [2 * H, L], F16)
        probs = sb("probs", [P, 2, 4, L], F32)
        oT = sb("oT", [P, 2, L], F32)
        recip = sb("recip", [P, 4, NT * 4], F32)
        tok = sb("tok", [P, NT, D], F32)
        cT_h = sb("cT_h", [P, KT, L], F16)
        cT_l = sb("cT_l", [P, KT, L], F16)
        x1 = sb("x1", [P, NT, D], F32)
        x1old = sb("x1old", [P, NT, D], F32)
        eh_h = sb("eh_h", [P, NE * MR, L], F16)
        eh_l = sb("eh_l", [P, NE * MR, L], F16)
        sh_h = sb("sh_h", [P, MS, L], F16)
        sh_l = sb("sh_l", [P, MS, L], F16)
        y = sb("y", [P, NT, D], F32)
        st6 = sb("st6", [P, 4, NT, 6], F32)
        mv = sb("mv", [P, 4, NT, 2], F32)
        veps = sb("veps", [P, 4, NT], F32)
        rstd = sb("rstd", [P, 4, NT], F32)
        carry = sb("carry", [P, 8], F32)
        gexp = sb("gexp", [P, NT, NE], F32)
        gs = sb("gs", [P, NT, NE], F32)
        gsel = sb("gsel", [P, NT, NE], F32)
        gtop = sb("gtop", [P, NT, NE], F32)
        gidx = sb("gidx", [P, NT, NE], U32)
        gidf = sb("gidf", [P, NT, 2], F32)
        gone = sb("gone", [P, 2, NT, NE], F32)
        gmask = sb("gmask", [P, NT, NE], F32)
        gss = sb("gss", [P, NT, NE], F32)
        gden = sb("gden", [P, 4, NT], F32)
        gtmp = sb("gtmp", [P, 2, NT, NE], F32)
        comb = sb("comb", [P, NT, NE], F32)

        psum = ctx.enter_context(nc.psum_tensor("psum", [P, 8 * L], F32))

        def pair(n):
            return psum[:, (n % 2) * 2 * L:(n % 2 + 1) * 2 * L]

        pv = psum[:, 4 * L:5 * L]

        def bank(n):
            return psum[:, (5 + n) * L:(6 + n) * L]

        w_loaded = [sem("w_loaded0"), sem("w_loaded1")]
        c_loaded = sem("c_loaded")
        c_made = sem("c_made")
        p_made = sem("p_made")
        w_hi_made = sem("w_hi_made")
        w_lo_made = sem("w_lo_made")
        x_loaded = sem("x_loaded")
        xres_loaded = sem("xres_loaded")
        x1_kept = sem("x1_kept")
        rep_done = [sem("rep_done0"), sem("rep_done1")]
        m_loaded = sem("m_loaded")
        stored = sem("stored")
        filled = [sem(f"filled{b}") for b in range(3)]
        emptied = [sem(f"emptied{b}") for b in range(3)]
        scores_full = sem("scores_full")
        scores_max = sem("scores_max")
        scoresT_full = sem("scoresT_full")
        exp_done = sem("exp_done")
        pv_done = sem("pv_done")
        oT_ready = sem("oT_ready")
        m_split = sem("m_split")
        xT_hi = sem("xT_hi")
        cT_hi = sem("cT_hi")
        rope_sum = sem("rope_sum")
        rope_hi = sem("rope_hi")
        rope_lo = sem("rope_lo")
        sh_hi = sem("sh_hi")
        h_lo = sem("h_lo")
        recip_ready = sem("recip_ready")
        ln_step = [sem(f"ln_step{k}") for k in "AOCF"]
        rstd_ready = [sem(f"rstd_ready{k}") for k in "AOCF"]
        applied = [sem(f"applied{k}") for k in "AOCF"]
        x1_ready = sem("x1_ready")
        y_ready = sem("y_ready")
        gate_step = sem("gate_step")
        A_, O_, C_, F_ = range(4)

        REP = 9 * 16
        NLN = 2 * NT + 1
        GST = 25

        block = ctx.enter_context(nc.Block())

        @block.sync
        def _(sp):
            for c in range(NCH):
                if c >= 2:
                    sp.wait_ge(w_lo_made, c - 1)
                sp.dma_start(probs[:, c % 2, :, :].rearrange("p a b -> p (a b)")[:, 0:CH],
                             wall[:, c * CH:(c + 1) * CH]).then_inc(w_loaded[c % 2], 16)
                if c == 1:
                    for dst, src in ((ident32[:, :], ident), (bqk_sb[:, :], bqk), (rows_sb[:, :], rows),
                                     (tabs_sb[:, :, :].rearrange("p a b -> p (a b)"), tabs), (iota_sb[:, :], iota)):
                        sp.dma_start(dst, src).then_inc(c_loaded, 16)

            def seq(ap, s, stage):
                n = s.i + SHIFT[stage]
                n = n if isinstance(n, int) else sp.snap(n)
                return ap[bass.ds(n, 1)].rearrange("o (p t) d -> p (o t) d", t=NT)

            def body(s):
                if s.has["a"]:
                    src = seq(x, s, "a")
                    if not s.first("a"):
                        sp.wait_ge(xT_hi, s.count("a", KT, 0))
                    sp.dma_start(xin[:, :, :], src).then_inc(x_loaded, 16)
                if s.has["d"]:
                    dst = seq(out, s, "d")
                    sp.wait_ge(y_ready, s.count("d", NT, NT))
                    sp.dma_start(dst, y[:, :, :]).then_inc(stored, 16)
                if s.has["c"]:
                    if not s.first("c"):
                        sp.wait_ge(y_ready, s.count("c", NT, 0))
                    sp.wait_ge(applied[C_], s.count("c", NT, NT))
                    sp.dma_start(x1old[:, :, :], x1[:, :, :]).then_inc(x1_kept, 16)
                if s.has["b"]:
                    src = seq(x, s, "b")
                    if not s.first("b"):
                        sp.wait_ge(x1_kept, s.count("b", 16, 0))
                    sp.dma_start(x1[:, :, :], src).then_inc(xres_loaded, 16)
                    sp.wait_ge(emptied[s.bank("MT")], s.nth("MT"))
                    for r in range(2):
                        sp.dma_start(qS[64 + r:65 + r, :, :], mrows[H * r:H * (r + 1), :]).then_inc(m_loaded, 16)
                if s.has["a"]:
                    for half in range(2):
                        hs = slice(8 * half, 8 * half + 8)
                        if s.has["b"]:
                            sp.wait_ge(scoresT_full, s.count("b", 2 * NQ, NQ * (half + 1)))
                        sp.dma_start(qS[64:66, hs, :], zeros).then_inc(rep_done[half], 16)
                        sp.wait_ge(rope_lo, s.count("a", 4, 2 * half + 2))
                        for r in range(4):
                            sp.dma_start(qS[DH * r:DH * (r + 1), hs, :],
                                         (rot_h, rot_l, rot_h, rot_l)[r][:, 0, half, :]).then_inc(rep_done[half], 16)
                            sp.dma_start(kS[DH * r:DH * (r + 1), hs, :],
                                         (rot_h, rot_h, rot_l, rot_l)[r][:, 1, half, :]).then_inc(rep_done[half], 16)

            walk(sp, body)
            sp.wait_ge(stored, 16 * NB)

        @block.tensor
        def _(pe):
            mm = nc.tensor.matmul

            def three(dst, terms):
                n = 3 * len(terms)
                k = 0
                for lh, ll, rh, rl in terms:
                    for a, b in ((lh, rh), (lh, rl), (ll, rh)):
                        last = mm(dst, a, b, start=(k == 0), stop=(k == n - 1))
                        k += 1
                return last

            def claim(s, item):
                if s.refills(item):
                    pe.wait_ge(emptied[s.bank(item)], s.nth(item) - 1)
                return bank(s.bank(item)), filled[s.bank(item)]

            def features(s, item, w0, width, kts, xh, xl):
                dst, sig = claim(s, item)
                three(dst, [(w_hi[:, w0 + kt * width:w0 + kt * width + P], w_lo[:, w0 + kt * width:w0 + kt * width + P],
                             xh[:, kt, :], xl[:, kt, :]) for kt in range(kts)]).then_inc(sig, 1)

            def tokens(s, item, tp, w0, kts, xh, xl, k0=0):
                dst, sig = claim(s, item)
                for u in range(2):
                    t = 2 * tp + u
                    last = three(dst[:, u * D:(u + 1) * D],
                                 [(xh[:, k0 + k, t * P:(t + 1) * P], xl[:, k0 + k, t * P:(t + 1) * P],
                                   w_hi[:, w0 + k * D:w0 + (k + 1) * D], w_lo[:, w0 + k * D:w0 + (k + 1) * D])
                                  for k in range(kts)])
                last.then_inc(sig, 1)

            def turned(s, item, src):
                dst, sig = claim(s, item)
                for t in range(NT):
                    last = nc.tensor.transpose(dst[:, t * P:(t + 1) * P], src(t), ident32[:, :])
                last.then_inc(sig, 1)

            def scores(s, n):
                h = n // 2
                if n % 16 == 0:
                    pe.wait_ge(rep_done[n // 16], s.count("b", REP, REP))
                if n >= 2:
                    pe.wait_ge(scores_max, s.count("b", NS, n - 1))
                elif not s.first("b"):
                    pe.wait_ge(exp_done, s.count("b", NS, n - 1))
                for u in range(2):
                    q0 = (2 * (n % 2) + u) * P
                    last = mm(pair(n)[:, u * L:(u + 1) * L], qS[0:KR, h, q0:q0 + P], kS[0:KR, h, :],
                              start=True, stop=True)
                last.then_inc(scores_full, 1)

            def scoresT(s, n, p):
                g, kt = n // 4, n % 4
                m = 2 * n + p
                if m == 0:
                    pe.wait_ge(m_loaded, s.count("b", 32, 32))
                if m < 2:
                    pe.wait_ge(scores_max, s.count("b", NS, NS - 1 + m))
                else:
                    pe.wait_ge(exp_done, s.count("b", NS, m - 1))
                for u in range(2):
                    h = 4 * g + 2 * p + u
                    last = mm(pair(m)[:, u * L:(u + 1) * L], kS[0:KR, h, kt * P:(kt + 1) * P], qS[0:KR, h, :],
                              start=True, stop=True)
                last.then_inc(scoresT_full, 1)

            def weighted(s, n):
                g, kt = n // 4, n % 4
                if n == 0:
                    pe.wait_ge(emptied[s.bank("V1")], s.nth("V1"))
                if kt == 0 and not (g == 0 and s.first("b")):
                    pe.wait_ge(oT_ready, s.count("b", 4, g))
                pe.wait_ge(exp_done, s.count("b", NS, 2 * n + 2))
                for j in range(4):
                    last = mm(pv[32 * j:32 * j + 32, :], vaug[:, kt, 4 * g + j, :], probs[:, n % 2, j, :],
                              start=(kt == 0), stop=(kt == 3))
                last.then_inc(pv_done, 1)

            def item_pe(s, item):
                if item[:2] == "OT":
                    g = int(item[2:])
                    pe.wait_ge(oT_ready, s.count(stage_of(item), 4, g + 1))
                    turned(s, item, lambda t: oT[:, g % 2, t * P:(t + 1) * P])
                elif item[:2] == "AT":
                    kt = int(item[2:])
                    pe.wait_ge(emptied[s.bank("OT3")], s.nth("OT3"))
                    turned(s, item, lambda t: tok[:, t, kt * P:(kt + 1) * P])
                elif item[:2] == "XT":
                    kt = int(item[2:])
                    pe.wait_ge(applied[C_], s.count("c", NT, NT))
                    turned(s, item, lambda t: tok[:, t, kt * P:(kt + 1) * P])
                elif item[:2] == "XA":
                    kt = int(item[2:])
                    pe.wait_ge(applied[A_], s.count("a", NT, NT))
                    turned(s, item, lambda t: xin[:, t, kt * P:(kt + 1) * P])
                elif item[0] == "V":
                    tokens(s, item, int(item[1:]), WV0, KT, xnT_h, xnT_l)
                elif item[:2] == "WO":
                    for kt in range(KT):
                        pe.wait_ge(emptied[s.bank(f"AT{kt}")], s.nth(f"AT{kt}"))
                    tokens(s, item, int(item[2:]), WO0, KT, cT_h, cT_l)
                elif item[:2] == "DS":
                    pe.wait_ge(h_lo, s.count("d", NE * MR + MS, NE * MR + MS))
                    tokens(s, item, int(item[2:]), SD0, MS, sh_h, sh_l)
                elif item[0] == "D":
                    e, tp = divmod(int(item[1:]), 2)
                    tokens(s, item, tp, ED0 + e * MR * D, MR, eh_h, eh_l, MR * e)
                elif item[0] == "U":
                    e, m = divmod(int(item[1:]), MR)
                    if item == "U0":
                        for kt in range(KT):
                            pe.wait_ge(emptied[s.bank(f"XT{kt}")], s.nth(f"XT{kt}"))
                    features(s, item, EU0 + e * KT * HR + m * P, HR, KT, cT_h, cT_l)
                elif item[0] == "S":
                    m, ab = divmod(int(item[1:]), 2)
                    features(s, item, (SA0, SB0)[ab] + m * P, HS, KT, cT_h, cT_l)
                elif item[0] == "Q":
                    n = int(item[1:])
                    half, w, ab = n // 4, n // 2 % 2, n % 2
                    if n == 0:
                        for kt in range(KT):
                            pe.wait_ge(emptied[s.bank(f"XA{kt}")], s.nth(f"XA{kt}"))
                    features(s, item, QK0 + (2 * w + ab) * D + half * P, 4 * D, KT, xnT_h, xnT_l)
                elif item == "RT":
                    dst, sig = claim(s, item)
                    for t in range(NT):
                        ts = slice(t * P, (t + 1) * P)
                        k = 0
                        for kt in range(KT):
                            rw = slice(RW0 + kt * NE, RW0 + (kt + 1) * NE)
                            for a, b in ((cT_h, w_hi), (cT_h, w_lo), (cT_l, w_hi), (cT_l, w_lo)):
                                last = mm(dst[:, t * NE:(t + 1) * NE], a[:, kt, ts], b[:, rw],
                                          start=(k == 0), stop=(k == 4 * KT - 1))
                                k += 1
                    last.then_inc(sig, 1)
                elif item == "MT":
                    dst, sig = claim(s, item)
                    pe.wait_ge(m_split, s.count("b", 2, 2))
                    half = dst[:, 0:L // 2].bitcast(F16)
                    for t in range(NT):
                        last = nc.tensor.transpose(half[0:2 * H, t * P:(t + 1) * P], mcols[:, t, :], ident16[:, :])
                    last.then_inc(sig, 1)

            pe.wait_ge(c_made, 2)
            pe.wait_ge(p_made, 3)
            pe.wait_ge(w_lo_made, NCH)

            def body(s):
                for tiles, item in first_half():
                    if s.has["b"]:
                        for n in tiles:
                            scores(s, n)
                    if s.has[stage_of(item)]:
                        item_pe(s, item)
                for n in range(NQ):
                    if s.has["b"]:
                        for p in range(2):
                            scoresT(s, n, p)
                        if n >= 1:
                            weighted(s, n - 1)
                    for item in BETWEEN.get(n, []):
                        if s.has[stage_of(item)]:
                            item_pe(s, item)
                if s.has["b"]:
                    weighted(s, NQ - 1)

            walk(pe, body)

        @block.scalar
        def _(act):
            A = nc.scalar.activation

            def item_act(s, item):
                if item[:2] in ("AT", "XT", "XA"):
                    kt = int(item[2:])
                    act.wait_ge(filled[s.bank(item)], s.nth(item))
                    src = bank(s.bank(item))
                    if item[:2] == "XA":
                        if s.has["b"]:
                            act.wait_ge(emptied[s.bank("V1")], s.nth("V1"))
                        A(xnT_h[:, kt, :], src, ACT.Identity).then_inc(xT_hi, 1)
                    else:
                        if item[:2] == "XT":
                            act.wait_ge(emptied[s.bank("WO1")], s.nth("WO1"))
                        A(cT_h[:, kt, :], src, ACT.Identity).then_inc(cT_hi, 1)
                elif item[:2] == "DS":
                    tp = int(item[2:])
                    act.wait_ge(filled[s.bank(item)], s.nth(item))
                    src = bank(s.bank(item))
                    if not s.first("d"):
                        act.wait_ge(stored, s.count("d", 16, 0))
                    A(y[:, 2 * tp:2 * tp + 2, :].rearrange("p a b -> p (a b)"), src, ACT.Identity,
                      scale=1.0 / WS).then_inc(emptied[s.bank(item)], 1)
                elif item[0] == "U":
                    n = int(item[1:])
                    act.wait_ge(filled[s.bank(item)], s.nth(item))
                    src = bank(s.bank(item))
                    if n >= 2 or not s.first("c"):
                        act.wait_ge(h_lo, s.count("c", NE * MR + MS, n - 1))
                    if n == 0:
                        act.wait_ge(rope_lo, s.count("b", 4, 4) if s.has["b"] else 4 * NB)
                    A(hid[:, n % 2, :], src, ACT.Gelu, scale=1.0 / WS)
                    A(eh_h[:, n, :], src, ACT.Gelu, scale=1.0 / WS).then_inc(emptied[s.bank(item)], 1)
                elif item[0] == "S":
                    m, ab = divmod(int(item[1:]), 2)
                    if ab == 0:
                        act.wait_ge(filled[s.bank(item)], s.nth(item))
                        src = bank(s.bank(item))
                        act.wait_ge(h_lo, s.count("c", NE * MR + MS, NE * MR + m - 1))
                        A(hid[:, m % 2, :], src, ACT.Silu, scale=1.0 / WS).then_inc(emptied[s.bank(item)], 1)
                    else:
                        act.wait_ge(emptied[s.bank(item)], s.nth(item))
                        A(sh_h[:, m, :], hid[:, m % 2, :], ACT.Identity).then_inc(sh_hi, 1)
                elif item[0] == "Q" and int(item[1:]) % 2:
                    n = int(item[1:]) // 2
                    half, w = divmod(n, 2)
                    act.wait_ge(rope_sum, s.count("a", 4, n + 1))
                    if n == 0 and not s.first("a"):
                        for r in range(2):
                            act.wait_ge(rep_done[r], s.count("a", REP, 0))
                    A(rot_h[:, w, half, :], rope[:, 0, :], ACT.Identity).then_inc(rope_hi, 1)
                elif item == "RT":
                    act.wait_ge(filled[s.bank(item)], s.nth(item))
                    src = bank(s.bank(item))
                    if not s.first("c"):
                        act.wait_ge(gate_step, s.count("c", GST, 0))
                    A(gexp[:, :, :].rearrange("p a b -> p (a b)"), src[:, 0:NT * NE], ACT.Exp,
                      scale=-1.0 / WS).then_inc(emptied[s.bank(item)], 1)

            def exps(s, n, p):
                m = 2 * n + p
                act.wait_ge(scoresT_full, s.count("b", NS, m + 1))
                if p == 0 and (n >= 2 or not s.first("b")):
                    act.wait_ge(pv_done, s.count("b", NQ, n - 1))
                A(probs[:, n % 2, 2 * p:2 * p + 2, :].rearrange("p a b -> p (a b)"), pair(m), ACT.Exp,
                  scale=SM).then_inc(exp_done, 1)

            def group_out(s, g):
                act.wait_ge(pv_done, s.count("b", NQ, 4 * g + 4))
                if g >= 2:
                    act.wait_ge(emptied[s.bank(f"OT{g - 2}")], s.nth(f"OT{g - 2}"))
                elif g == 1 and s.has["c"]:
                    act.wait_ge(emptied[s.bank("OT3")], s.nth("OT3"))
                A(oT[:, g % 2, :], pv, ACT.Identity).then_inc(oT_ready, 1)

            for c in range(NCH):
                act.wait_ge(w_loaded[c % 2], 16 * (c // 2 + 1))
                A(w_hi[:, c * CH:(c + 1) * CH], probs[:, c % 2, :, :].rearrange("p a b -> p (a b)")[:, 0:CH],
                  ACT.Identity, scale=WS).then_inc(w_hi_made, 1)

            def body(s):
                for _, item in first_half():
                    if s.has[stage_of(item)]:
                        item_act(s, item)
                for n in range(NQ):
                    if s.has["b"]:
                        for p in range(2):
                            exps(s, n, p)
                        if n >= 4 and n % 4 == 0:
                            group_out(s, n // 4 - 1)
                    for item in BETWEEN.get(n, []):
                        if s.has[stage_of(item)]:
                            item_act(s, item)
                if s.has["b"]:
                    group_out(s, 3)

            walk(act, body)

        @block.gpsimd
        def _(pool):
            TT = nc.gpsimd.tensor_tensor
            nc.gpsimd.memset(vaug[:, :, :, :], 1.0).then_inc(p_made, 1)
            pool.wait_ge(p_made, 1)
            nc.gpsimd.memset(kS[64:66, :, :], 1.0).then_inc(p_made, 1)
            pool.wait_ge(p_made, 2)
            nc.gpsimd.memset(minus_half[:, :], -0.5).then_inc(p_made, 1)
            pool.wait_ge(p_made, 3)

            def item_pool(s, item):
                if item[:2] == "LN" and item[3] == "1":
                    k = "AOCF".index(item[2])
                    pool.wait_ge(ln_step[k], s.count(stage_of(item), NLN, NLN))
                    TT(rstd[:, k, :], veps[:, k, :], minus_half[:, :], ALU.pow).then_inc(rstd_ready[k], 1)
                elif item[0] == "U":
                    n = int(item[1:])
                    pool.wait_ge(emptied[s.bank(item)], s.nth(item))
                    TT(eh_l[:, n, :], hid[:, n % 2, :], eh_h[:, n, :], ALU.subtract).then_inc(h_lo, 1)
                elif item[0] == "S" and int(item[1:]) % 2:
                    m = int(item[1:]) // 2
                    pool.wait_ge(sh_hi, s.count("c", MS, m + 1))
                    TT(sh_l[:, m, :], hid[:, m % 2, :], sh_h[:, m, :], ALU.subtract).then_inc(h_lo, 1)
                elif item[0] == "Q" and int(item[1:]) % 2:
                    n = int(item[1:]) // 2
                    half, w = divmod(n, 2)
                    pool.wait_ge(emptied[s.bank(f"Q{2 * n}")], s.nth(f"Q{2 * n}"))
                    pool.wait_ge(emptied[s.bank(item)], s.nth(item))
                    TT(rope[:, 0, :], rope[:, 0, :], rope[:, 1, :], ALU.add).then_inc(rope_sum, 1)
                    pool.wait_ge(rope_hi, s.count("a", 4, n + 1))
                    TT(rot_l[:, w, half, :], rope[:, 0, :], rot_h[:, w, half, :], ALU.subtract).then_inc(rope_lo, 1)

            def body(s):
                for _, item in first_half():
                    if s.has[stage_of(item)]:
                        item_pool(s, item)
                for n in range(NQ):
                    for item in BETWEEN.get(n, []):
                        if s.has[stage_of(item)]:
                            item_pool(s, item)

            walk(pool, body)

        @block.vector
        def _(dve):
            V = nc.vector

            def norm_stats(s, k, src):
                st = "acc d".replace(" ", "")[k]
                c = lambda n: s.count(st, NLN, n)
                for t in range(NT):
                    V.bn_stats(st6[:, k, t, :], src[:, t, :]).then_inc(ln_step[k], 1)
                dve.wait_ge(ln_step[k], c(NT))
                V.memset(carry[:, k:k + 1], 0.0)
                for t in range(NT):
                    V.bn_aggr(mv[:, k, t, :], st6[:, k, t, :]).then_inc(ln_step[k], 1)
                dve.wait_ge(ln_step[k], c(2 * NT))
                V.tensor_scalar(veps[:, k, :], mv[:, k, :, 1], EPS, None, ALU.add).then_inc(ln_step[k], 1)

            def norm_apply(s, k, dst, src):
                st = "accd"[k]
                dve.wait_ge(rstd_ready[k], s.count(st, 1, 1))
                for t in range(NT):
                    V.tensor_scalar(dst[:, t, :], src[:, t, :], mv[:, k, t, 0:1], rstd[:, k, t:t + 1],
                                    ALU.subtract, ALU.mult).then_inc(applied[k], 1)

            def gates(s):
                k = [0]

                def step(ins):
                    k[0] += 1
                    ins.then_inc(gate_step, 1)
                    dve.wait_ge(gate_step, s.count("c", GST, k[0]))

                flat = lambda a: a.rearrange("p a b -> p (a b)")
                step(V.tensor_scalar(flat(gss[:, :, :]), flat(gexp[:, :, :]), 1.0, None, ALU.add))
                step(V.reciprocal(flat(gs[:, :, :]), flat(gss[:, :, :])))
                k[0] += 1
                V.tensor_tensor(gsel[:, :, :], gs[:, :, :], rb_b.unsqueeze(1).broadcast_to([P, NT, NE]),
                                ALU.add).then_inc(gate_step, 1)
                dve.wait_ge(gate_step, s.count("c", GST, k[0]))
                V.memset(carry[:, 4:5], 0.0)
                for t in range(NT):
                    k[0] += 1
                    V.max(gtop[:, t, :], gsel[:, t, :]).then_inc(gate_step, 1)
                dve.wait_ge(gate_step, s.count("c", GST, k[0]))
                V.memset(carry[:, 5:6], 0.0)
                for t in range(NT):
                    k[0] += 1
                    V.max_index(gidx[:, t, :], gtop[:, t, :], gsel[:, t, :]).then_inc(gate_step, 1)
                dve.wait_ge(gate_step, s.count("c", GST, k[0]))
                step(V.tensor_copy(gidf[:, :, :], gidx[:, :, 0:2]))
                for c in range(2):
                    k[0] += 1
                    V.tensor_tensor(gone[:, c, :, :], iota_sb[:, :].unsqueeze(1).broadcast_to([P, NT, NE]),
                                    gidf[:, :, c:c + 1].broadcast_to([P, NT, NE]), ALU.is_equal).then_inc(gate_step, 1)
                dve.wait_ge(gate_step, s.count("c", GST, k[0]))
                step(V.tensor_tensor(gmask[:, :, :], gone[:, 0, :, :], gone[:, 1, :, :], ALU.add))
                step(V.tensor_tensor(gss[:, :, :], gmask[:, :, :], gs[:, :, :], ALU.mult))
                step(V.tensor_reduce(gden[:, 0, :], gss[:, :, :], axis=AX.X, op=ALU.add))
                step(V.tensor_scalar(gden[:, 1, :], gden[:, 0, :], 1e-9, 1.0 / WS, ALU.is_gt, ALU.mult))
                step(V.tensor_scalar(gden[:, 2, :], gden[:, 0, :], 1e-9, None, ALU.add))
                step(V.reciprocal(gden[:, 3, :], gden[:, 2, :]))
                step(V.tensor_tensor(gden[:, 3, :], gden[:, 3, :], gden[:, 1, :], ALU.mult))
                step(V.tensor_scalar(gden[:, 2, :], gden[:, 1, :], -0.5, 0.5 / WS, ALU.mult, ALU.add))
                for c, (a, b) in enumerate(((gss, 3), (gmask, 2))):
                    k[0] += 1
                    V.tensor_tensor(gtmp[:, c, :, :], a[:, :, :],
                                    gden[:, b, :].unsqueeze(2).broadcast_to([P, NT, NE]), ALU.mult).then_inc(gate_step, 1)
                dve.wait_ge(gate_step, s.count("c", GST, k[0]))
                step(V.tensor_tensor(comb[:, :, :], gtmp[:, 0, :, :], gtmp[:, 1, :, :], ALU.add))
                assert k[0] == GST, k[0]

            def item_dve(s, item):
                if uses_bank(item):
                    done = emptied[s.bank(item)]
                if item[:2] == "OT":
                    g = int(item[2:])
                    dve.wait_ge(filled[s.bank(item)], s.nth(item))
                    src = bank(s.bank(item))
                    if item == "OT0" and s.has["c"]:
                        dve.wait_ge(emptied[s.bank("XT1")], s.nth("XT1"))
                    stage = stage_of(item)
                    v = src.rearrange("p (a c) -> p a c", c=32)
                    V.reciprocal(recip[:, g, :], v[:, :, DH]).then_inc(recip_ready, 1)
                    dve.wait_ge(recip_ready, s.count(stage, 4, g + 1))
                    V.tensor_tensor(tok[:, :, 64 * g:64 * g + 64].rearrange("p t (j c) -> p t j c", c=DH),
                                    src.rearrange("p (t j c) -> p t j c", t=NT, c=32)[:, :, :, 0:DH],
                                    recip[:, g, :].rearrange("p (t j) -> p t j", t=NT).unsqueeze(3)
                                    .broadcast_to([P, NT, 4, DH]), ALU.mult).then_inc(done, 1)
                elif item[:2] in ("AT", "XT", "XA"):
                    kt = int(item[2:])
                    dve.wait_ge(filled[s.bank(item)], s.nth(item))
                    src = bank(s.bank(item))
                    if item[:2] == "XA":
                        dve.wait_ge(xT_hi, s.count("a", KT, kt + 1))
                        V.tensor_tensor(xnT_l[:, kt, :], src, xnT_h[:, kt, :], ALU.subtract).then_inc(done, 1)
                    else:
                        dve.wait_ge(cT_hi, s.count("c", 2 * KT, kt + 1 + (KT if item[:2] == "XT" else 0)))
                        V.tensor_tensor(cT_l[:, kt, :], src, cT_h[:, kt, :], ALU.subtract).then_inc(done, 1)
                elif item[0] == "V":
                    tp = int(item[1:])
                    dve.wait_ge(filled[s.bank(item)], s.nth(item))
                    src = bank(s.bank(item))
                    if tp == 0 and not s.first("b"):
                        dve.wait_ge(oT_ready, s.count("b", 4, 0))
                    for u in range(2):
                        last = V.scalar_tensor_tensor(vaug[:, 2 * tp + u, :, 0:DH],
                                                      src[:, u * D:(u + 1) * D].rearrange("p (h c) -> p h c", c=DH),
                                                      1.0 / WS, bv_b.rearrange("p (h c) -> p h c", c=DH),
                                                      ALU.mult, ALU.add)
                    last.then_inc(done, 1)
                elif item[:2] == "WO":
                    tp = int(item[2:])
                    dve.wait_ge(filled[s.bank(item)], s.nth(item))
                    src = bank(s.bank(item))
                    for u in range(2):
                        last = V.scalar_tensor_tensor(tok[:, 2 * tp + u, :], src[:, u * D:(u + 1) * D], 1.0 / WS, bo_b,
                                                      ALU.mult, ALU.add)
                    last.then_inc(done, 1)
                elif item == "LNO1":
                    for tp in range(2):
                        dve.wait_ge(emptied[s.bank(f"WO{tp}")], s.nth(f"WO{tp}"))
                    norm_stats(s, O_, tok)
                elif item == "LNO2":
                    norm_apply(s, O_, tok, tok)
                    dve.wait_ge(applied[O_], s.count("c", NT, NT))
                    dve.wait_ge(xres_loaded, s.count("c", 16, 16))
                    for t in range(NT):
                        V.tensor_tensor(x1[:, t, :], x1[:, t, :], tok[:, t, :], ALU.add).then_inc(x1_ready, 1)
                elif item == "LNC1":
                    dve.wait_ge(x1_ready, s.count("c", NT, NT))
                    norm_stats(s, C_, x1)
                elif item == "LNC2":
                    norm_apply(s, C_, tok, x1)
                elif item[:2] == "DS":
                    pass
                elif item[0] == "D":
                    n = int(item[1:])
                    e, tp = divmod(n, 2)
                    dve.wait_ge(filled[s.bank(item)], s.nth(item))
                    src = bank(s.bank(item))
                    so_far = f"D{n - 2}" if n >= 2 else f"DS{tp}"
                    dve.wait_ge(emptied[s.bank(so_far)], s.nth(so_far))
                    for u in range(2):
                        t = 2 * tp + u
                        last = V.scalar_tensor_tensor(y[:, t, :], src[:, u * D:(u + 1) * D], comb[:, t, e:e + 1],
                                                      y[:, t, :], ALU.mult, ALU.add)
                    last.then_inc(done, 1)
                elif item == "LNF1":
                    for n in (14, 15):
                        dve.wait_ge(emptied[s.bank(f"D{n}")], s.nth(f"D{n}"))
                    norm_stats(s, F_, y)
                elif item == "LNF2":
                    norm_apply(s, F_, y, y)
                    dve.wait_ge(applied[F_], s.count("d", NT, NT))
                    dve.wait_ge(x1_kept, s.count("d", 16, 16))
                    for t in range(NT):
                        V.tensor_tensor(y[:, t, :], y[:, t, :], x1old[:, t, :], ALU.add).then_inc(y_ready, 1)
                elif item == "LNA1":
                    dve.wait_ge(x_loaded, s.count("a", 16, 16))
                    norm_stats(s, A_, xin)
                elif item == "LNA2":
                    norm_apply(s, A_, xin, xin)
                elif item[0] == "S" and int(item[1:]) % 2:
                    m = int(item[1:]) // 2
                    dve.wait_ge(filled[s.bank(item)], s.nth(item))
                    src = bank(s.bank(item))
                    dve.wait_ge(emptied[s.bank(f"S{2 * m}")], s.nth(f"S{2 * m}"))
                    V.scalar_tensor_tensor(hid[:, m % 2, :], hid[:, m % 2, :], 1.0 / WS, src, ALU.mult,
                                           ALU.mult).then_inc(done, 1)
                elif item[0] == "Q":
                    n = int(item[1:])
                    half, w, ab = n // 4, n // 2 % 2, n % 2
                    dve.wait_ge(filled[s.bank(item)], s.nth(item))
                    src = bank(s.bank(item))
                    if ab == 0 and (n > 0 or not s.first("a")):
                        dve.wait_ge(rope_lo, s.count("a", 4, n // 2))
                    if n == 0 and s.has["c"]:
                        dve.wait_ge(h_lo, s.count("c", NE * MR + MS, NE * MR + MS))
                    b = (w * 2 + ab) * 2 + half
                    V.scalar_tensor_tensor(rope[:, ab, :], src, bqk_sb[:, b:b + 1], tabs_sb[:, ab, :], ALU.add,
                                           ALU.mult).then_inc(done, 1)
                elif item == "GATE":
                    dve.wait_ge(emptied[s.bank("RT")], s.nth("RT"))
                    gates(s)
                elif item == "MT":
                    dve.wait_ge(scores_max, s.count("b", NS, NS))
                    V.tensor_copy(mcols[:, :, 0:H], negm[:, :, :]).then_inc(m_split, 1)
                    dve.wait_ge(m_split, s.count("b", 2, 1))
                    V.tensor_tensor(mcols[:, :, H:2 * H], negm[:, :, :], mcols[:, :, 0:H],
                                    ALU.subtract).then_inc(m_split, 1)
                    dve.wait_ge(filled[s.bank(item)], s.nth(item))
                    src = bank(s.bank(item))
                    if not s.first("b"):
                        dve.wait_ge(m_loaded, s.count("b", 32, 0))
                    V.tensor_copy(mrows[:, :], src[:, 0:L // 2].bitcast(F16)[0:2 * H, :]).then_inc(done, 1)

            def maxima(s, n):
                h, qp = divmod(n, 2)
                dve.wait_ge(scores_full, s.count("b", NS, n + 1))
                if n == 0 and not s.first("b"):
                    dve.wait_ge(m_split, s.count("b", 2, 0))
                V.tensor_reduce(negm[:, 2 * qp:2 * qp + 2, h], pair(n).rearrange("p (a b) -> p a b", b=L), axis=AX.X,
                                op=ALU.max, negate=True).then_inc(scores_max, 1)

            dve.wait_ge(c_loaded, 16 * 5)
            V.tensor_copy(ident16[:, :], ident32[:, :]).then_inc(c_made, 1)
            V.tensor_scalar(bqk_sb[:, :], bqk_sb[:, :], WS, None, ALU.mult).then_inc(c_made, 1)
            dve.wait_ge(c_made, 2)
            dve.wait_ge(p_made, 3)
            for c in range(NCH):
                dve.wait_ge(w_hi_made, c + 1)
                cols = slice(c * CH, (c + 1) * CH)
                V.scalar_tensor_tensor(w_lo[:, cols], probs[:, c % 2, :, :].rearrange("p a b -> p (a b)")[:, 0:CH],
                                       WS, w_hi[:, cols], ALU.mult, ALU.subtract).then_inc(w_lo_made, 1)

            def body(s):
                for tiles, item in first_half():
                    if s.has["b"]:
                        for n in tiles:
                            maxima(s, n)
                    if s.has[stage_of(item)]:
                        item_dve(s, item)
                for n in range(NQ):
                    for item in BETWEEN.get(n, []):
                        if s.has[stage_of(item)]:
                            item_dve(s, item)

            walk(dve, body)


_PARAMS = ["x", "wall", "bqk", "rows", "tabs", "iota", "ident", "zeros"]


def kernel(L0_attn_x, L0_attn_Wq, L0_attn_bq, L0_attn_Wk, L0_attn_bk, L0_attn_Wv, L0_attn_bv, L0_attn_Wo, L0_attn_bo,
           L0_ffn_router_w, L0_ffn_router_bias, L0_ffn_sw1, L0_ffn_sw3, L0_ffn_sw2, L0_ffn_ew1, L0_ffn_ew2):
    import numpy as np
    import concourse.bacc as bacc
    from concourse import mybir as mb
    from concourse.bass_utils import run_bass_kernel_spmd

    a = np.asarray
    order = np.array([[[(8 * hf + hh) * DH + j for hh in range(8)] for j in range(DH)] for hf in range(2)]).ravel()
    swapped = np.array([f // DH * DH + (f % DH + DH // 2) % DH for f in order])

    def rows_on_partitions(w):
        return w.reshape(-1, P, w.shape[-1]).transpose(1, 0, 2).reshape(P, -1)

    qT, kT = a(L0_attn_Wq).T, a(L0_attn_Wk).T
    wqk = np.concatenate([qT[:, order], qT[:, swapped], kT[:, order], kT[:, swapped]], axis=1)
    parts = [wqk, a(L0_attn_Wv).T, a(L0_attn_Wo).T, a(L0_ffn_sw1), a(L0_ffn_sw3), a(L0_ffn_sw2)]
    parts += [a(L0_ffn_ew1)[e] for e in range(NE)] + [a(L0_ffn_ew2)[e] for e in range(NE)] + [a(L0_ffn_router_w).T]
    wall = np.concatenate([rows_on_partitions(w) for w in parts], axis=1)
    bq, bk = a(L0_attn_bq), a(L0_attn_bk)
    bqk = np.stack([b[o].reshape(2, P)[hf] for b in (bq, bk) for o in (order, swapped) for hf in range(2)], axis=1)
    rows = np.concatenate([np.broadcast_to(a(r)[None, :], (P, a(r).shape[0]))
                           for r in (L0_attn_bv, L0_attn_bo, L0_ffn_router_bias)], axis=1)
    inv = (np.float32(1.0) / np.power(np.float32(10000.0), np.arange(0, DH, 2, dtype=np.float32) / np.float32(DH)))
    pos = np.array([NT * p + t for t in range(NT) for p in range(P)], np.float32)
    ang = (pos[None, :] * inv[:, None].astype(np.float32)).astype(np.float64)
    j = np.arange(P) // 8
    sign = np.where(j < DH // 2, -1.0, 1.0)[:, None]
    tabs = np.concatenate([np.cos(ang)[j % 8] / WS, sign * np.sin(ang)[j % 8] / WS], axis=1).astype(np.float32)
    iota = np.broadcast_to(np.arange(NE, dtype=np.float32)[None, :], (P, NE))
    ident = np.eye(P, dtype=np.float32)
    zeros = np.zeros((2, 8 * L), np.float16)
    arrays = dict(x=a(L0_attn_x), wall=wall, bqk=bqk, rows=rows, tabs=tabs, iota=iota, ident=ident, zeros=zeros)
    arrays = {k: np.ascontiguousarray(v) for k, v in arrays.items()}

    nc = bacc.Bacc("TRN2", target_bir_lowering=False, num_devices=1)
    args = [nc.dram_tensor(f"{k}_dram", arrays[k].shape, mb.dt.from_np(arrays[k].dtype), kind="ExternalInput").ap()
            for k in _PARAMS]
    args.append(nc.dram_tensor("out_dram", (NB, L, D), mb.dt.float32, kind="ExternalOutput").ap())
    block_program(nc, *args)
    r = run_bass_kernel_spmd(nc, [{f"{k}_dram": v for k, v in arrays.items()}], core_ids=[0])
    return r.results[0]["out_dram"]
```

```python
import concourse.bass as bass
from concourse import mybir
from contextlib import ExitStack

F32 = mybir.dt.float32
F16 = mybir.dt.float16
U32 = mybir.dt.uint32
ACT = mybir.ActivationFunctionType
ALU = mybir.AluOpType
AX = mybir.AxisListType

NB, L, D = 32, 512, 256
H, DH = 16, 16
HS, HR, NE = 512, 256, 8
P = 128
NT = L // P
KT = D // P
MS = HS // P
MR = HR // P
EPS = 1e-5
WS = 64.0
SM = float(DH) ** -0.5

QK0 = 0
WV0 = QK0 + KT * 2 * D
WO0 = WV0 + KT * D
SA0 = WO0 + KT * D
SB0 = SA0 + KT * HS
SD0 = SB0 + KT * HS
EU0 = SD0 + MS * D
ED0 = EU0 + NE * KT * HR
RW0 = ED0 + NE * MR * D
WCOLS = RW0 + KT * NE
NCH = 7
CH = WCOLS // NCH
assert CH * NCH == WCOLS and CH <= 4 * L

NS = H * 2
NQ = 16
KR = 66

FIRST_HALF = (
    "OT3", "D2", "D3", "AT0", "AT1", "D4", "WO0", "WO1", "D5", "LNO1", "D6", "D7", "LNO2", "D8", "LNC1", "D9",
    "D10", "D11", "D12", "LNC2", "D13", "XT0", "XT1", "D14", "RT", "D15", "U0", "LNF1", "U1", "U2", "LNF2", "U3",
    "U4", "U5", "U6", "U7", "U8", "U9", "U10", "U11", "U12", "U13", "U14", "U15", "S0", "S1", "MC", "S2", "S3",
    "S4", "MT", "S5", "S6", "LNA1", "S7"
)
BETWEEN = {0: ["V0", "V1"], 1: ["GX"], 2: ["LNA2", "XA0"], 3: ["DS0", "XA1"], 4: ["Q0", "DS1"], 5: ["OT0"],
           7: ["GATE"], 8: ["Q1"], 9: ["Q2"], 10: ["OT1"], 11: ["D0"], 12: ["Q3"], 14: ["OT2"], 15: ["D1"]}
EARLY = ("DS0", "DS1", "D0", "D1")
SCORES_AT = "1110011100100100000101011010011012121111211120000000000"


def stage_of(item):
    if item[:2] in ("OT",):
        return "c" if item == "OT3" else "b"
    if item[0] == "V" or item in ("MC", "MT"):
        return "b"
    if item in EARLY:
        return "c"
    if item[0] == "D" or item[:3] == "LNF":
        return "d"
    if item[:2] == "XA" or item[0] == "Q" or item[:3] == "LNA":
        return "a"
    return "c"


SHIFT = {"a": 1, "b": 0, "c": -1, "d": -2}
LATER_ODD = range(3, 2 * NE, 2)
USES_BANK = ("OT", "V", "DS", "AT", "D", "WO", "XT", "U", "S", "MT", "XA", "RT", "Q")


def uses_bank(item):
    return not item.startswith("LN") and item not in ("GATE", "GX", "MC")


def first_half():
    done = 0
    for n, item in enumerate(FIRST_HALF):
        upto = done + int(SCORES_AT[n])
        yield range(done, upto), item
        done = upto
    assert done == NS


class Step:

    def __init__(self, i, at, base, per):
        self.i, self.at, self.base, self.per = i, at, base, per
        self.has = {s: 0 <= at + SHIFT[s] < NB for s in SHIFT}
        self.plan, self.used = {}, [0, 0, 0]
        order = [x for _, x in first_half()] + [x for n in range(NQ) for x in BETWEEN.get(n, [])]
        n = 0
        for item in order:
            if uses_bank(item) and self.has[stage_of(item)]:
                self.plan[item] = (n % 3, self.used[n % 3])
                self.used[n % 3] += 1
                n += 1

    def count(self, stage, per, c):
        return self.i * per + (SHIFT[stage] * per + c)

    def first(self, stage):
        return self.at + SHIFT[stage] == 0

    def bank(self, item):
        return self.plan[item][0]

    def nth(self, item):
        bank, nth = self.plan[item]
        n = self.base[bank] + nth + 1
        return n if self.per is None else self.i * self.per[bank] + (n - self.at * self.per[bank])

    def refills(self, item):
        return self.base[self.plan[item][0]] + self.plan[item][1] > 0


def steps():
    base, out = [0, 0, 0], []
    for at in range(-1, NB + 2):
        s = Step(at, at, list(base), None)
        out.append(s)
        base = [b + u for b, u in zip(base, s.used)]
    return out


LOOP = (2, NB - 2)


def walk(eng, body):
    every = steps()
    for s in every:
        if s.at < LOOP[0] or s.at > LOOP[1]:
            body(s)
        elif s.at == LOOP[0]:
            with eng.Fori(LOOP[0], LOOP[1] + 1) as i:
                body(Step(i, s.at, s.base, list(s.used)))


def block_program(nc, x, wall, bqk, rows, tabs, iota, ident, zeros, out):
    ctx = ExitStack()
    with ctx:
        def sb(name, shape, dt):
            return ctx.enter_context(nc.sbuf_tensor(name, shape, dt))

        def sem(name):
            return ctx.enter_context(nc.semaphore(name))

        w_hi = sb("w_hi", [P, WCOLS], F16)
        w_lo = sb("w_lo", [P, WCOLS], F16)
        w_router = sb("w_router", [P, KT, 2 * NE], F16)
        ident32 = sb("ident32", [P, P], F32)
        ident16 = sb("ident16", [P, P], F16)
        bqk_sb = sb("bqk_sb", [P, 4], F32)
        rows_sb = sb("rows_sb", [P, 2 * D + NE], F32)
        tabs_sb = sb("tabs_sb", [P, 2, L], F32)
        iota_sb = sb("iota_sb", [P, NE], F32)
        minus_half = sb("minus_half", [P, NT], F32)
        bv_b, bo_b, rb_b = rows_sb[:, 0:D], rows_sb[:, D:2 * D], rows_sb[:, 2 * D:]

        xin = sb("xin", [P, NT, D], F32)
        xnT_h = sb("xnT_h", [P, KT, L], F16)
        xnT_l = sb("xnT_l", [P, KT, L], F16)
        rope = sb("rope", [P, 2, L], F32)
        hid = rope
        rot_h = sb("rot_h", [P, 2, 2, L], F16)
        rot_l = sb("rot_l", [P, 2, 2, L], F16)
        qS = sb("qS", [P, H, L], F16)
        kS = sb("kS", [P, H, L], F16)
        vaug = sb("vaug", [P, NT, H, 32], F32)
        negm = sb("negm", [P, NT, H], F32)
        mcols = sb("mcols", [P, NT, 2 * H], F16)
        mrows = sb("mrows", [2 * H, L], F16)
        probs = sb("probs", [P, 2, 4, L], F32)
        oT = sb("oT", [P, 2, L], F32)
        recip = sb("recip", [P, 4, NT * 4], F32)
        tok = sb("tok", [P, NT, D], F32)
        cT_h = sb("cT_h", [P, KT, L], F16)
        cT_l = sb("cT_l", [P, KT, L], F16)
        x1 = sb("x1", [P, NT, D], F32)
        x1old = sb("x1old", [P, NT, D], F32)
        eh_h = sb("eh_h", [P, NE * MR, L], F16)
        eh_l = sb("eh_l", [P, NE * MR, L], F16)
        sh_h = sb("sh_h", [P, MS, L], F16)
        sh_l = sb("sh_l", [P, MS, L], F16)
        y = sb("y", [P, NT, D], F32)
        st6 = sb("st6", [P, 4, NT, 6], F32)
        mv = sb("mv", [P, 4, NT, 2], F32)
        veps = sb("veps", [P, 4, NT], F32)
        rstd = sb("rstd", [P, 4, NT], F32)
        negmean = sb("negmean", [P, 4, NT], F32)
        shift = sb("shift", [P, 4, NT], F32)
        carry = sb("carry", [P, 8], F32)
        logits = sb("logits", [P, NT, NE], F32)
        gexp = sb("gexp", [P, NT, NE], F32)
        gs = sb("gs", [P, NT, NE], F32)
        gsel = sb("gsel", [P, NT, NE], F32)
        gtop = sb("gtop", [P, NT, NE], F32)
        gidx = sb("gidx", [P, NT, NE], U32)
        gidf = sb("gidf", [P, NT, 2], F32)
        gone = sb("gone", [P, 2, NT, NE], F32)
        gmask = sb("gmask", [P, NT, NE], F32)
        gss = sb("gss", [P, NT, NE], F32)
        gden = sb("gden", [P, 4, NT], F32)
        gtmp = sb("gtmp", [P, 2, NT, NE], F32)
        comb = sb("comb", [P, NT, NE], F32)

        psum = ctx.enter_context(nc.psum_tensor("psum", [P, 8 * L], F32))

        def pair(n):
            return psum[:, (n % 2) * 2 * L:(n % 2 + 1) * 2 * L]

        pv = psum[:, 4 * L:5 * L]

        def bank(n):
            return psum[:, (5 + n) * L:(6 + n) * L]

        w_loaded = [sem("w_loaded0"), sem("w_loaded1")]
        c_loaded = sem("c_loaded")
        c_made = sem("c_made")
        p_made = sem("p_made")
        w_hi_made = sem("w_hi_made")
        w_lo_made = sem("w_lo_made")
        w_router_made = sem("w_router_made")
        x_loaded = sem("x_loaded")
        xres_loaded = sem("xres_loaded")
        x1_kept = sem("x1_kept")
        rep_done = [sem("rep_done0"), sem("rep_done1")]
        m_loaded = sem("m_loaded")
        stored = sem("stored")
        filled = [sem(f"filled{b}") for b in range(3)]
        emptied = [sem(f"emptied{b}") for b in range(3)]
        scores_full = sem("scores_full")
        scores_max = sem("scores_max")
        scoresT_full = sem("scoresT_full")
        exp_done = sem("exp_done")
        pv_done = sem("pv_done")
        oT_ready = sem("oT_ready")
        m_split = sem("m_split")
        xT_hi = sem("xT_hi")
        cT_hi = sem("cT_hi")
        rope_sum = sem("rope_sum")
        rope_hi = sem("rope_hi")
        rope_lo = sem("rope_lo")
        sh_hi = sem("sh_hi")
        h_lo = sem("h_lo")
        recip_ready = sem("recip_ready")
        ln_step = [sem(f"ln_step{k}") for k in "AOCF"]
        rstd_ready = [sem(f"rstd_ready{k}") for k in "AOCF"]
        applied = [sem(f"applied{k}") for k in "AOCF"]
        x1_ready = sem("x1_ready")
        y_ready = sem("y_ready")
        y_added = sem("y_added")
        gexp_made = sem("gexp_made")
        gate_step = sem("gate_step")
        A_, O_, C_, F_ = range(4)

        REP = 9 * 16
        NLN = 2 * NT + 2
        GST = 25

        block = ctx.enter_context(nc.Block())

        @block.sync
        def _(sp):

            def seq(ap, s, stage):
                n = s.i + SHIFT[stage]
                n = n if isinstance(n, int) else sp.snap(n)
                return ap[bass.ds(n, 1)].rearrange("o (p t) d -> p (o t) d", t=NT)

            def body(s):
                if s.has["a"]:
                    src = seq(x, s, "a")
                    if not s.first("a"):
                        sp.wait_ge(xT_hi, s.count("a", KT, 0))
                    sp.dma_start(xin[:, :, :], src).then_inc(x_loaded, 16)
                if s.at == -1:
                    for dst, src in ((ident32[:, :], ident), (bqk_sb[:, :], bqk), (rows_sb[:, :], rows),
                                     (tabs_sb[:, :, :].rearrange("p a b -> p (a b)"), tabs), (iota_sb[:, :], iota)):
                        sp.dma_start(dst, src).then_inc(c_loaded, 16)
                if s.has["b"]:
                    sp.wait_ge(emptied[s.bank("MT")], s.nth("MT"))
                    for r in range(2):
                        sp.dma_start(qS[64 + r:65 + r, :, :], mrows[H * r:H * (r + 1), :]).then_inc(m_loaded, 16)
                if s.has["d"]:
                    dst = seq(out, s, "d")
                    sp.wait_ge(y_ready, s.count("d", 1, 1))
                    sp.dma_start(dst, y[:, :, :]).then_inc(stored, 16)
                if s.has["c"]:
                    sp.wait_ge(applied[C_], s.count("c", NT, NT))
                    sp.dma_start(x1old[:, :, :], x1[:, :, :]).then_inc(x1_kept, 16)
                if s.has["b"]:
                    src = seq(x, s, "b")
                    if not s.first("b"):
                        sp.wait_ge(x1_kept, s.count("b", 16, 0))
                    sp.dma_start(x1[:, :, :], src).then_inc(xres_loaded, 16)
                if s.has["a"]:
                    for half in range(2):
                        hs = slice(8 * half, 8 * half + 8)
                        if s.has["b"]:
                            sp.wait_ge(scoresT_full, s.count("b", 2 * NQ, NQ * (half + 1)))
                        sp.dma_start(qS[64:66, hs, :], zeros).then_inc(rep_done[half], 16)
                        sp.wait_ge(rope_lo, s.count("a", 4, 2 * half + 2))
                        for r in range(4):
                            sp.dma_start(qS[DH * r:DH * (r + 1), hs, :],
                                         (rot_h, rot_l, rot_h, rot_l)[r][:, 0, half, :]).then_inc(rep_done[half], 16)
                            sp.dma_start(kS[DH * r:DH * (r + 1), hs, :],
                                         (rot_h, rot_h, rot_l, rot_l)[r][:, 1, half, :]).then_inc(rep_done[half], 16)

            walk(sp, body)
            sp.wait_ge(stored, 16 * NB)

        @block.tensor
        def _(pe):
            mm = nc.tensor.matmul

            def three(dst, terms):
                n = 3 * len(terms)
                k = 0
                for lh, ll, rh, rl in terms:
                    for a, b in ((lh, rh), (lh, rl), (ll, rh)):
                        last = mm(dst, a, b, start=(k == 0), stop=(k == n - 1))
                        k += 1
                return last

            def claim(s, item):
                if s.refills(item):
                    pe.wait_ge(emptied[s.bank(item)], s.nth(item) - 1)
                return bank(s.bank(item)), filled[s.bank(item)]

            def features(s, item, w0, width, kts, xh, xl):
                dst, sig = claim(s, item)
                three(dst, [(w_hi[:, w0 + kt * width:w0 + kt * width + P], w_lo[:, w0 + kt * width:w0 + kt * width + P],
                             xh[:, kt, :], xl[:, kt, :]) for kt in range(kts)]).then_inc(sig, 1)

            def tokens(s, item, tp, w0, kts, xh, xl, k0=0):
                dst, sig = claim(s, item)
                for u in range(2):
                    t = 2 * tp + u
                    last = three(dst[:, u * D:(u + 1) * D],
                                 [(xh[:, k0 + k, t * P:(t + 1) * P], xl[:, k0 + k, t * P:(t + 1) * P],
                                   w_hi[:, w0 + k * D:w0 + (k + 1) * D], w_lo[:, w0 + k * D:w0 + (k + 1) * D])
                                  for k in range(kts)])
                last.then_inc(sig, 1)

            def turned(s, item, src):
                dst, sig = claim(s, item)
                for t in range(NT):
                    if item == "XT0":
                        pe.wait_ge(applied[C_], s.count("c", NT, t + 1))
                    last = nc.tensor.transpose(dst[:, t * P:(t + 1) * P], src(t), ident32[:, :])
                last.then_inc(sig, 1)

            def scores(s, n):
                h = n // 2
                if n % 16 == 0:
                    pe.wait_ge(rep_done[n // 16], s.count("b", REP, REP))
                if n >= 2:
                    pe.wait_ge(scores_max, s.count("b", NS, n - 1))
                elif not s.first("b"):
                    pe.wait_ge(exp_done, s.count("b", NS, n - 1))
                for u in range(2):
                    q0 = (2 * (n % 2) + u) * P
                    last = mm(pair(n)[:, u * L:(u + 1) * L], qS[0:KR, h, q0:q0 + P], kS[0:KR, h, :],
                              start=True, stop=True)
                last.then_inc(scores_full, 1)

            def scoresT(s, n, p):
                g, kt = n // 4, n % 4
                m = 2 * n + p
                if m == 0:
                    pe.wait_ge(m_loaded, s.count("b", 32, 32))
                if m < 2:
                    pe.wait_ge(scores_max, s.count("b", NS, NS - 1 + m))
                else:
                    pe.wait_ge(exp_done, s.count("b", NS, m - 1))
                for u in range(2):
                    h = 4 * g + 2 * p + u
                    last = mm(pair(m)[:, u * L:(u + 1) * L], kS[0:KR, h, kt * P:(kt + 1) * P], qS[0:KR, h, :],
                              start=True, stop=True)
                last.then_inc(scoresT_full, 1)

            def weighted(s, n):
                g, kt = n // 4, n % 4
                if n == 0:
                    pe.wait_ge(emptied[s.bank("V1")], s.nth("V1"))
                if kt == 0 and not (g == 0 and s.first("b")):
                    pe.wait_ge(oT_ready, s.count("b", 4, g))
                pe.wait_ge(exp_done, s.count("b", NS, 2 * n + 2))
                for j in range(4):
                    last = mm(pv[32 * j:32 * j + 32, :], vaug[:, kt, 4 * g + j, :], probs[:, n % 2, j, :],
                              start=(kt == 0), stop=(kt == 3))
                last.then_inc(pv_done, 1)

            def item_pe(s, item):
                if item[:2] == "OT":
                    g = int(item[2:])
                    pe.wait_ge(oT_ready, s.count(stage_of(item), 4, g + 1))
                    turned(s, item, lambda t: oT[:, g % 2, t * P:(t + 1) * P])
                elif item[:2] == "AT":
                    kt = int(item[2:])
                    pe.wait_ge(emptied[s.bank("OT3")], s.nth("OT3"))
                    turned(s, item, lambda t: tok[:, t, kt * P:(kt + 1) * P])
                elif item[:2] == "XT":
                    kt = int(item[2:])
                    turned(s, item, lambda t: tok[:, t, kt * P:(kt + 1) * P])
                elif item[:2] == "XA":
                    kt = int(item[2:])
                    pe.wait_ge(applied[A_], s.count("a", NT, NT))
                    turned(s, item, lambda t: xin[:, t, kt * P:(kt + 1) * P])
                elif item[0] == "V":
                    tokens(s, item, int(item[1:]), WV0, KT, xnT_h, xnT_l)
                elif item[:2] == "WO":
                    for kt in range(KT):
                        pe.wait_ge(emptied[s.bank(f"AT{kt}")], s.nth(f"AT{kt}"))
                    tokens(s, item, int(item[2:]), WO0, KT, cT_h, cT_l)
                elif item[:2] == "DS":
                    pe.wait_ge(h_lo, s.count("c", NE * MR + MS, NE * MR + MS))
                    tokens(s, item, int(item[2:]), SD0, MS, sh_h, sh_l)
                elif item[0] == "D":
                    e, tp = divmod(int(item[1:]), 2)
                    tokens(s, item, tp, ED0 + e * MR * D, MR, eh_h, eh_l, MR * e)
                elif item[0] == "U":
                    e, m = divmod(int(item[1:]), MR)
                    features(s, item, EU0 + e * KT * HR + m * P, HR, KT, cT_h, cT_l)
                elif item[0] == "S":
                    m, ab = divmod(int(item[1:]), 2)
                    features(s, item, (SA0, SB0)[ab] + m * P, HS, KT, cT_h, cT_l)
                elif item[0] == "Q":
                    n = int(item[1:])
                    half, w = divmod(n, 2)
                    if s.at == -1:
                        pe.wait_ge(w_lo_made, 1)
                    if n == 0:
                        for kt in range(KT):
                            pe.wait_ge(emptied[s.bank(f"XA{kt}")], s.nth(f"XA{kt}"))
                    features(s, item, QK0 + w * D + half * P, 2 * D, KT, xnT_h, xnT_l)
                elif item == "RT":
                    for kt in range(KT):
                        pe.wait_ge(emptied[s.bank(f"XT{kt}")], s.nth(f"XT{kt}"))
                    dst, sig = claim(s, item)
                    for t in range(NT):
                        for kt in range(KT):
                            for a in (cT_h, cT_l):
                                last = mm(dst[:, 2 * NE * t:2 * NE * (t + 1)], a[:, kt, t * P:(t + 1) * P],
                                          w_router[:, kt, :], start=(kt == 0 and a is cT_h),
                                          stop=(kt == KT - 1 and a is cT_l))
                    last.then_inc(sig, 1)
                elif item == "MT":
                    dst, sig = claim(s, item)
                    pe.wait_ge(m_split, s.count("b", 2, 2))
                    half = dst[:, 0:L // 2].bitcast(F16)
                    for t in range(NT):
                        last = nc.tensor.transpose(half[0:2 * H, t * P:(t + 1) * P], mcols[:, t, :], ident16[:, :])
                    last.then_inc(sig, 1)

            pe.wait_ge(c_made, 2)
            assert WO0 <= CH

            def body(s):
                if s.at == 0:
                    pe.wait_ge(p_made, 3)
                if s.at == 1:
                    pe.wait_ge(w_lo_made, NCH)
                    pe.wait_ge(w_router_made, 2)
                for tiles, item in first_half():
                    if s.has["b"]:
                        for n in tiles:
                            scores(s, n)
                    if s.has[stage_of(item)]:
                        item_pe(s, item)
                for n in range(NQ):
                    if s.has["b"]:
                        for p in range(2):
                            scoresT(s, n, p)
                        if n >= 1:
                            weighted(s, n - 1)
                    for item in BETWEEN.get(n, []):
                        if s.has[stage_of(item)]:
                            item_pe(s, item)
                if s.has["b"]:
                    weighted(s, NQ - 1)

            walk(pe, body)

        @block.scalar
        def _(act):
            A = nc.scalar.activation

            def item_act(s, item):
                if item in ("LNO2", "LNC2", "LNF2"):
                    k = "AOCF".index(item[2])
                    dst, src = {"O": (tok, tok), "C": (tok, x1), "F": (y, y)}[item[2]]
                    act.wait_ge(rstd_ready[k], s.count(stage_of(item), 2, 2))
                    for t in range(NT):
                        A(dst[:, t, :], src[:, t, :], ACT.Identity, scale=rstd[:, k, t:t + 1],
                          bias=shift[:, k, t:t + 1]).then_inc(applied[k], 1)
                if item[:2] in ("AT", "XT", "XA"):
                    kt = int(item[2:])
                    act.wait_ge(filled[s.bank(item)], s.nth(item))
                    src = bank(s.bank(item))
                    if item[:2] == "XA":
                        if s.has["b"]:
                            act.wait_ge(emptied[s.bank("V1")], s.nth("V1"))
                        A(xnT_h[:, kt, :], src, ACT.Identity).then_inc(xT_hi, 1)
                    else:
                        if item[:2] == "XT":
                            act.wait_ge(emptied[s.bank("WO1")], s.nth("WO1"))
                        elif not s.first("c"):
                            act.wait_ge(h_lo, s.count("c", NE * MR + MS, 0))
                        A(cT_h[:, kt, :], src, ACT.Identity).then_inc(cT_hi, 1)
                elif item[:2] == "DS":
                    tp = int(item[2:])
                    act.wait_ge(filled[s.bank(item)], s.nth(item))
                    src = bank(s.bank(item))
                    if not s.first("c"):
                        act.wait_ge(stored, s.count("c", 16, 0))
                    A(y[:, 2 * tp:2 * tp + 2, :].rearrange("p a b -> p (a b)"), src, ACT.Identity,
                      scale=1.0 / WS).then_inc(emptied[s.bank(item)], 1)
                elif item[0] == "D" and int(item[1:]) in LATER_ODD:
                    k = LATER_ODD.index(int(item[1:]))
                    act.wait_ge(filled[s.bank(item)], s.nth(item))
                    src = bank(s.bank(item))
                    if k >= 2:
                        act.wait_ge(y_added, s.count("d", len(LATER_ODD), k - 1))
                    for u in range(2):
                        last = A(oT[:, k % 2, u * D:(u + 1) * D], src[:, u * D:(u + 1) * D], ACT.Identity,
                                 scale=comb[:, 2 + u, k + 1:k + 2])
                    last.then_inc(emptied[s.bank(item)], 1)
                elif item[0] == "U":
                    n = int(item[1:])
                    act.wait_ge(filled[s.bank(item)], s.nth(item))
                    src = bank(s.bank(item))
                    if n >= 2 or not s.first("c"):
                        act.wait_ge(h_lo, s.count("c", NE * MR + MS, n - 1))
                    if n == 0:
                        act.wait_ge(rope_lo, s.count("b", 4, 4) if s.has["b"] else 4 * NB)
                    A(hid[:, n % 2, :], src, ACT.Gelu, scale=1.0 / WS)
                    A(eh_h[:, n, :], src, ACT.Gelu, scale=1.0 / WS).then_inc(emptied[s.bank(item)], 1)
                elif item[0] == "S":
                    m, ab = divmod(int(item[1:]), 2)
                    if ab == 0:
                        act.wait_ge(filled[s.bank(item)], s.nth(item))
                        src = bank(s.bank(item))
                        act.wait_ge(h_lo, s.count("c", NE * MR + MS, NE * MR + m - 1))
                        A(hid[:, m % 2, :], src, ACT.Silu, scale=1.0 / WS).then_inc(emptied[s.bank(item)], 1)
                elif item == "GX":
                    act.wait_ge(emptied[s.bank("RT")], s.nth("RT"))
                    if not s.first("c"):
                        act.wait_ge(gate_step, s.count("c", GST, 0))
                    A(gexp[:, :, :].rearrange("p a b -> p (a b)"), logits[:, :, :].rearrange("p a b -> p (a b)"),
                      ACT.Exp, scale=-1.0 / WS).then_inc(gexp_made, 1)

            def exps(s, n, p):
                m = 2 * n + p
                act.wait_ge(scoresT_full, s.count("b", NS, m + 1))
                if p == 0 and (n >= 2 or not s.first("b")):
                    act.wait_ge(pv_done, s.count("b", NQ, n - 1))
                A(probs[:, n % 2, 2 * p:2 * p + 2, :].rearrange("p a b -> p (a b)"), pair(m), ACT.Exp,
                  scale=SM).then_inc(exp_done, 1)

            def group_out(s, g):
                act.wait_ge(pv_done, s.count("b", NQ, 4 * g + 4))
                if g < 2 and s.has["d"]:
                    act.wait_ge(y_added, s.count("d", len(LATER_ODD), len(LATER_ODD)))
                if g >= 2:
                    act.wait_ge(emptied[s.bank(f"OT{g - 2}")], s.nth(f"OT{g - 2}"))
                elif g == 1 and s.has["c"]:
                    act.wait_ge(emptied[s.bank("OT3")], s.nth("OT3"))
                A(oT[:, g % 2, :], pv, ACT.Identity).then_inc(oT_ready, 1)

            def load_weights(c):
                act.dma_start(probs[:, c % 2, :, :].rearrange("p a b -> p (a b)")[:, 0:CH],
                              wall[:, c * CH:(c + 1) * CH]).then_inc(w_loaded[c % 2], 16)

            def weights(c):
                act.wait_ge(w_loaded[c % 2], 16 * (c // 2 + 1))
                A(w_hi[:, c * CH:(c + 1) * CH], probs[:, c % 2, :, :].rearrange("p a b -> p (a b)")[:, 0:CH],
                  ACT.Identity, scale=WS).then_inc(w_hi_made, 1)
                if c >= 1 and c + 1 < NCH:
                    act.wait_ge(w_lo_made, c)
                    load_weights(c + 1)

            load_weights(0)
            load_weights(1)

            def body(s):
                if s.at == 0:
                    for c in range(1, NCH):
                        weights(c)
                for _, item in first_half():
                    if s.has[stage_of(item)]:
                        item_act(s, item)
                for n in range(NQ):
                    if s.has["b"]:
                        for p in range(2):
                            exps(s, n, p)
                        if n >= 4 and n % 4 == 0:
                            group_out(s, n // 4 - 1)
                    for item in BETWEEN.get(n, []):
                        if s.has[stage_of(item)]:
                            item_act(s, item)
                if s.at == -1:
                    weights(0)
                if s.has["b"]:
                    group_out(s, 3)

            walk(act, body)

        @block.gpsimd
        def _(pool):
            TT = nc.gpsimd.tensor_tensor

            def flat(a):
                return a[:, :, :].rearrange("p a b -> p (a b)")

            nc.gpsimd.memset(minus_half[:, :], -0.5).then_inc(p_made, 1)
            pool.wait_ge(p_made, 1)
            nc.gpsimd.memset(kS[64:66, :, :], 1.0).then_inc(p_made, 1)
            pool.wait_ge(p_made, 2)
            nc.gpsimd.memset(vaug[:, :, :, :], 1.0).then_inc(p_made, 1)
            pool.wait_ge(p_made, 3)

            def item_pool(s, item):
                if item[:2] == "LN" and item[3] == "1":
                    k = "AOCF".index(item[2])
                    pool.wait_ge(ln_step[k], s.count(stage_of(item), NLN, NLN))
                    TT(rstd[:, k, :], veps[:, k, :], minus_half[:, :], ALU.pow).then_inc(rstd_ready[k], 1)
                    pool.wait_ge(rstd_ready[k], s.count(stage_of(item), 2, 1))
                    TT(shift[:, k, :], negmean[:, k, :], rstd[:, k, :], ALU.mult).then_inc(rstd_ready[k], 1)
                elif item == "LNO2":
                    pool.wait_ge(xres_loaded, s.count("c", 16, 16))
                    for t in range(NT):
                        pool.wait_ge(applied[O_], s.count("c", NT, t + 1))
                        TT(x1[:, t, :], x1[:, t, :], tok[:, t, :], ALU.add).then_inc(x1_ready, 1)
                elif item == "LNF2":
                    pool.wait_ge(applied[F_], s.count("d", NT, NT))
                    pool.wait_ge(x1_kept, s.count("d", 16, 16))
                    TT(flat(y), flat(y), flat(x1old), ALU.add).then_inc(y_ready, 1)
                elif item[0] == "D" and item[:2] != "DS" and int(item[1:]) in LATER_ODD:
                    k = LATER_ODD.index(int(item[1:]))
                    pool.wait_ge(emptied[s.bank(item)], s.nth(item))
                    if k >= 1:
                        pool.wait_ge(y_added, s.count("d", len(LATER_ODD), k))
                    half = y[:, 2:4, :].rearrange("p a b -> p (a b)")
                    TT(half, half, oT[:, k % 2, :], ALU.add).then_inc(y_added, 1)
                elif item[0] == "U":
                    n = int(item[1:])
                    pool.wait_ge(emptied[s.bank(item)], s.nth(item))
                    TT(eh_l[:, n, :], hid[:, n % 2, :], eh_h[:, n, :], ALU.subtract).then_inc(h_lo, 1)
                elif item[0] == "S" and int(item[1:]) % 2:
                    m = int(item[1:]) // 2
                    pool.wait_ge(sh_hi, s.count("c", MS, m + 1))
                    TT(sh_l[:, m, :], hid[:, m % 2, :], sh_h[:, m, :], ALU.subtract).then_inc(h_lo, 1)

            def body(s):
                for _, item in first_half():
                    if s.has[stage_of(item)]:
                        item_pool(s, item)
                for n in range(NQ):
                    for item in BETWEEN.get(n, []):
                        if s.has[stage_of(item)]:
                            item_pool(s, item)

            walk(pool, body)

        @block.vector
        def _(dve):
            V = nc.vector

            def norm_stats(s, k, src):
                st = "acc d".replace(" ", "")[k]
                c = lambda n: s.count(st, NLN, n)
                for t in range(NT):
                    if k == C_:
                        dve.wait_ge(x1_ready, s.count("c", NT, t + 1))
                    V.bn_stats(st6[:, k, t, :], src[:, t, :]).then_inc(ln_step[k], 1)
                dve.wait_ge(ln_step[k], c(NT))
                V.memset(carry[:, k:k + 1], 0.0)
                for t in range(NT):
                    V.bn_aggr(mv[:, k, t, :], st6[:, k, t, :]).then_inc(ln_step[k], 1)
                dve.wait_ge(ln_step[k], c(2 * NT))
                V.tensor_scalar(negmean[:, k, :], mv[:, k, :, 0], -1.0, None, ALU.mult).then_inc(ln_step[k], 1)
                V.tensor_scalar(veps[:, k, :], mv[:, k, :, 1], EPS, None, ALU.add).then_inc(ln_step[k], 1)

            def norm_apply(s, k, dst, src):
                st = "accd"[k]
                dve.wait_ge(rstd_ready[k], s.count(st, 2, 2))
                for t in range(NT):
                    V.tensor_scalar(dst[:, t, :], src[:, t, :], mv[:, k, t, 0:1], rstd[:, k, t:t + 1],
                                    ALU.subtract, ALU.mult).then_inc(applied[k], 1)

            def gates(s):
                k = [0]

                def step(ins):
                    k[0] += 1
                    ins.then_inc(gate_step, 1)
                    dve.wait_ge(gate_step, s.count("c", GST, k[0]))

                flat = lambda a: a.rearrange("p a b -> p (a b)")
                step(V.tensor_scalar(flat(gss[:, :, :]), flat(gexp[:, :, :]), 1.0, None, ALU.add))
                step(V.reciprocal(flat(gs[:, :, :]), flat(gss[:, :, :])))
                k[0] += 1
                V.tensor_tensor(gsel[:, :, :], gs[:, :, :], rb_b.unsqueeze(1).broadcast_to([P, NT, NE]),
                                ALU.add).then_inc(gate_step, 1)
                dve.wait_ge(gate_step, s.count("c", GST, k[0]))
                V.memset(carry[:, 4:5], 0.0)
                for t in range(NT):
                    k[0] += 1
                    V.max(gtop[:, t, :], gsel[:, t, :]).then_inc(gate_step, 1)
                dve.wait_ge(gate_step, s.count("c", GST, k[0]))
                V.memset(carry[:, 5:6], 0.0)
                for t in range(NT):
                    k[0] += 1
                    V.max_index(gidx[:, t, :], gtop[:, t, :], gsel[:, t, :]).then_inc(gate_step, 1)
                dve.wait_ge(gate_step, s.count("c", GST, k[0]))
                step(V.tensor_copy(gidf[:, :, :], gidx[:, :, 0:2]))
                for c in range(2):
                    k[0] += 1
                    V.tensor_tensor(gone[:, c, :, :], iota_sb[:, :].unsqueeze(1).broadcast_to([P, NT, NE]),
                                    gidf[:, :, c:c + 1].broadcast_to([P, NT, NE]), ALU.is_equal).then_inc(gate_step, 1)
                dve.wait_ge(gate_step, s.count("c", GST, k[0]))
                step(V.tensor_tensor(gmask[:, :, :], gone[:, 0, :, :], gone[:, 1, :, :], ALU.add))
                step(V.tensor_tensor(gss[:, :, :], gmask[:, :, :], gs[:, :, :], ALU.mult))
                step(V.tensor_reduce(gden[:, 0, :], gss[:, :, :], axis=AX.X, op=ALU.add))
                step(V.tensor_scalar(gden[:, 1, :], gden[:, 0, :], 1e-9, 1.0 / WS, ALU.is_gt, ALU.mult))
                step(V.tensor_scalar(gden[:, 2, :], gden[:, 0, :], 1e-9, None, ALU.add))
                step(V.reciprocal(gden[:, 3, :], gden[:, 2, :]))
                step(V.tensor_tensor(gden[:, 3, :], gden[:, 3, :], gden[:, 1, :], ALU.mult))
                step(V.tensor_scalar(gden[:, 2, :], gden[:, 1, :], -0.5, 0.5 / WS, ALU.mult, ALU.add))
                for c, (a, b) in enumerate(((gss, 3), (gmask, 2))):
                    k[0] += 1
                    V.tensor_tensor(gtmp[:, c, :, :], a[:, :, :],
                                    gden[:, b, :].unsqueeze(2).broadcast_to([P, NT, NE]), ALU.mult).then_inc(gate_step, 1)
                dve.wait_ge(gate_step, s.count("c", GST, k[0]))
                step(V.tensor_tensor(comb[:, :, :], gtmp[:, 0, :, :], gtmp[:, 1, :, :], ALU.add))
                assert k[0] == GST, k[0]

            def weights(c):
                dve.wait_ge(w_hi_made, c + 1)
                cols = slice(c * CH, (c + 1) * CH)
                V.scalar_tensor_tensor(w_lo[:, cols], probs[:, c % 2, :, :].rearrange("p a b -> p (a b)")[:, 0:CH],
                                       WS, w_hi[:, cols], ALU.mult, ALU.subtract).then_inc(w_lo_made, 1)

            def constants():
                dve.wait_ge(c_loaded, 16 * 5)
                V.tensor_copy(ident16[:, :], ident32[:, :]).then_inc(c_made, 1)
                V.tensor_scalar(bqk_sb[:, :], bqk_sb[:, :], WS, None, ALU.mult).then_inc(c_made, 1)
                dve.wait_ge(c_made, 2)

            def item_dve(s, item):
                if s.at == -1 and item == "XA0":
                    constants()
                if s.at == -1 and item == "Q0":
                    weights(0)
                if uses_bank(item):
                    done = emptied[s.bank(item)]
                if item[:2] == "OT":
                    g = int(item[2:])
                    dve.wait_ge(filled[s.bank(item)], s.nth(item))
                    src = bank(s.bank(item))
                    if item == "OT0" and s.has["c"]:
                        dve.wait_ge(emptied[s.bank("XT1")], s.nth("XT1"))
                    stage = stage_of(item)
                    v = src.rearrange("p (a c) -> p a c", c=32)
                    V.reciprocal(recip[:, g, :], v[:, :, DH]).then_inc(recip_ready, 1)
                    dve.wait_ge(recip_ready, s.count(stage, 4, g + 1))
                    V.tensor_tensor(tok[:, :, 64 * g:64 * g + 64].rearrange("p t (j c) -> p t j c", c=DH),
                                    src.rearrange("p (t j c) -> p t j c", t=NT, c=32)[:, :, :, 0:DH],
                                    recip[:, g, :].rearrange("p (t j) -> p t j", t=NT).unsqueeze(3)
                                    .broadcast_to([P, NT, 4, DH]), ALU.mult).then_inc(done, 1)
                elif item[:2] in ("AT", "XT", "XA"):
                    kt = int(item[2:])
                    dve.wait_ge(filled[s.bank(item)], s.nth(item))
                    src = bank(s.bank(item))
                    if item[:2] == "XA":
                        dve.wait_ge(xT_hi, s.count("a", KT, kt + 1))
                        V.tensor_tensor(xnT_l[:, kt, :], src, xnT_h[:, kt, :], ALU.subtract).then_inc(done, 1)
                    else:
                        dve.wait_ge(cT_hi, s.count("c", 2 * KT, kt + 1 + (KT if item[:2] == "XT" else 0)))
                        V.tensor_tensor(cT_l[:, kt, :], src, cT_h[:, kt, :], ALU.subtract).then_inc(done, 1)
                elif item[0] == "V":
                    tp = int(item[1:])
                    dve.wait_ge(filled[s.bank(item)], s.nth(item))
                    src = bank(s.bank(item))
                    if tp == 0 and not s.first("b"):
                        dve.wait_ge(oT_ready, s.count("b", 4, 0))
                    for u in range(2):
                        last = V.scalar_tensor_tensor(vaug[:, 2 * tp + u, :, 0:DH],
                                                      src[:, u * D:(u + 1) * D].rearrange("p (h c) -> p h c", c=DH),
                                                      1.0 / WS, bv_b.rearrange("p (h c) -> p h c", c=DH),
                                                      ALU.mult, ALU.add)
                    last.then_inc(done, 1)
                elif item[:2] == "WO":
                    tp = int(item[2:])
                    dve.wait_ge(filled[s.bank(item)], s.nth(item))
                    src = bank(s.bank(item))
                    for u in range(2):
                        last = V.scalar_tensor_tensor(tok[:, 2 * tp + u, :], src[:, u * D:(u + 1) * D], 1.0 / WS, bo_b,
                                                      ALU.mult, ALU.add)
                    last.then_inc(done, 1)
                elif item == "LNO1":
                    for tp in range(2):
                        dve.wait_ge(emptied[s.bank(f"WO{tp}")], s.nth(f"WO{tp}"))
                    norm_stats(s, O_, tok)
                elif item == "LNC1":
                    norm_stats(s, C_, x1)
                elif item[:2] == "DS" or (item[0] == "D" and int(item[1:]) in LATER_ODD):
                    pass
                elif item[0] == "D":
                    n = int(item[1:])
                    e, tp = divmod(n, 2)
                    dve.wait_ge(filled[s.bank(item)], s.nth(item))
                    src = bank(s.bank(item))
                    so_far = f"D{n - 2}" if n >= 2 else f"DS{tp}"
                    if so_far not in EARLY or item in EARLY:
                        dve.wait_ge(emptied[s.bank(so_far)], s.nth(so_far))
                    for u in range(2):
                        t = 2 * tp + u
                        last = V.scalar_tensor_tensor(y[:, t, :], src[:, u * D:(u + 1) * D], comb[:, t, e:e + 1],
                                                      y[:, t, :], ALU.mult, ALU.add)
                    last.then_inc(done, 1)
                elif item == "LNF1":
                    dve.wait_ge(emptied[s.bank("D14")], s.nth("D14"))
                    dve.wait_ge(y_added, s.count("d", len(LATER_ODD), len(LATER_ODD)))
                    norm_stats(s, F_, y)
                elif item == "LNA1":
                    dve.wait_ge(x_loaded, s.count("a", 16, 16))
                    norm_stats(s, A_, xin)
                elif item == "LNA2":
                    norm_apply(s, A_, xin, xin)
                elif item[0] == "S" and int(item[1:]) % 2:
                    m = int(item[1:]) // 2
                    dve.wait_ge(filled[s.bank(item)], s.nth(item))
                    src = bank(s.bank(item))
                    dve.wait_ge(emptied[s.bank(f"S{2 * m}")], s.nth(f"S{2 * m}"))
                    V.scalar_tensor_tensor(hid[:, m % 2, :], hid[:, m % 2, :], 1.0 / WS, src, ALU.mult,
                                           ALU.mult).then_inc(done, 1)
                    dve.wait_ge(emptied[s.bank(item)], s.nth(item))
                    V.tensor_copy(sh_h[:, m, :], hid[:, m % 2, :]).then_inc(sh_hi, 1)
                elif item[0] == "Q":
                    n = int(item[1:])
                    half, w = divmod(n, 2)
                    dve.wait_ge(filled[s.bank(item)], s.nth(item))
                    src = bank(s.bank(item))
                    if n == 0 and s.has["c"]:
                        dve.wait_ge(h_lo, s.count("c", NE * MR + MS, NE * MR + MS))
                    if n > 0 or not s.first("a"):
                        dve.wait_ge(rope_lo, s.count("a", 4, n))
                    b = slice(2 * w + half, 2 * w + half + 1)
                    V.scalar_tensor_tensor(rope[:, 0, :], src, bqk_sb[:, b], tabs_sb[:, 0, :], ALU.add, ALU.mult)
                    for to, of in ((0, P // 2), (P // 2, 0)):
                        last = V.scalar_tensor_tensor(rope[to:to + P // 2, 1, :], src[of:of + P // 2, :],
                                                      bqk_sb[of:of + P // 2, b], tabs_sb[of:of + P // 2, 1, :],
                                                      ALU.add, ALU.mult)
                    last.then_inc(done, 1)
                    dve.wait_ge(emptied[s.bank(item)], s.nth(item))
                    V.tensor_tensor(rope[:, 0, :], rope[:, 0, :], rope[:, 1, :], ALU.add).then_inc(rope_sum, 1)
                    dve.wait_ge(rope_sum, s.count("a", 4, n + 1))
                    if n == 0 and not s.first("a"):
                        for r in range(2):
                            dve.wait_ge(rep_done[r], s.count("a", REP, 0))
                    V.tensor_copy(rot_h[:, w, half, :], rope[:, 0, :]).then_inc(rope_hi, 1)
                    dve.wait_ge(rope_hi, s.count("a", 4, n + 1))
                    V.tensor_tensor(rot_l[:, w, half, :], rope[:, 0, :], rot_h[:, w, half, :],
                                    ALU.subtract).then_inc(rope_lo, 1)
                elif item == "RT":
                    dve.wait_ge(filled[s.bank(item)], s.nth(item))
                    if not s.first("c"):
                        dve.wait_ge(gexp_made, s.count("c", 1, 0))
                    V.tensor_reduce(logits[:, :, :], bank(s.bank(item))[:, 0:2 * NT * NE]
                                    .rearrange("p (t h n) -> p t n h", t=NT, h=2), axis=AX.X,
                                    op=ALU.add).then_inc(done, 1)
                elif item == "GATE":
                    dve.wait_ge(gexp_made, s.count("c", 1, 1))
                    gates(s)
                elif item == "MC":
                    dve.wait_ge(scores_max, s.count("b", NS, NS))
                    V.tensor_copy(mcols[:, :, 0:H], negm[:, :, :]).then_inc(m_split, 1)
                    dve.wait_ge(m_split, s.count("b", 2, 1))
                    V.tensor_tensor(mcols[:, :, H:2 * H], negm[:, :, :], mcols[:, :, 0:H],
                                    ALU.subtract).then_inc(m_split, 1)
                elif item == "MT":
                    dve.wait_ge(filled[s.bank(item)], s.nth(item))
                    src = bank(s.bank(item))
                    if not s.first("b"):
                        dve.wait_ge(m_loaded, s.count("b", 32, 0))
                    V.tensor_copy(mrows[:, :], src[:, 0:L // 2].bitcast(F16)[0:2 * H, :]).then_inc(done, 1)

            assert NS // 5 == NCH - 1

            def maxima(s, n):
                h, qp = divmod(n, 2)
                dve.wait_ge(scores_full, s.count("b", NS, n + 1))
                if n == 0 and not s.first("b"):
                    dve.wait_ge(m_split, s.count("b", 2, 0))
                if s.at == 0 and n % 5 == 4:
                    weights(n // 5 + 1)
                    if n // 5 + 1 == NCH - 1:
                        dve.wait_ge(w_lo_made, NCH)
                        for k, w in enumerate((w_hi, w_lo)):
                            V.tensor_copy(w_router[:, :, NE * k:NE * (k + 1)],
                                          w[:, RW0:].rearrange("p (k n) -> p k n", k=KT)).then_inc(w_router_made, 1)
                V.tensor_reduce(negm[:, 2 * qp:2 * qp + 2, h], pair(n).rearrange("p (a b) -> p a b", b=L), axis=AX.X,
                                op=ALU.max, negate=True).then_inc(scores_max, 1)

            def body(s):
                if s.at == 0:
                    dve.wait_ge(p_made, 3)
                for tiles, item in first_half():
                    if s.has["b"]:
                        for n in tiles:
                            maxima(s, n)
                    if s.has[stage_of(item)]:
                        item_dve(s, item)
                for n in range(NQ):
                    for item in BETWEEN.get(n, []):
                        if s.has[stage_of(item)]:
                            item_dve(s, item)

            walk(dve, body)


_PARAMS = ["x", "wall", "bqk", "rows", "tabs", "iota", "ident", "zeros"]


def kernel(L0_attn_x, L0_attn_Wq, L0_attn_bq, L0_attn_Wk, L0_attn_bk, L0_attn_Wv, L0_attn_bv, L0_attn_Wo, L0_attn_bo,
           L0_ffn_router_w, L0_ffn_router_bias, L0_ffn_sw1, L0_ffn_sw3, L0_ffn_sw2, L0_ffn_ew1, L0_ffn_ew2):
    import numpy as np
    import concourse.bacc as bacc
    from concourse import mybir as mb
    from concourse.bass_utils import run_bass_kernel_spmd

    a = np.asarray
    order = np.array([[[(8 * hf + hh) * DH + j for hh in range(8)] for j in range(DH)] for hf in range(2)]).ravel()

    def rows_on_partitions(w):
        return w.reshape(-1, P, w.shape[-1]).transpose(1, 0, 2).reshape(P, -1)

    qT, kT = a(L0_attn_Wq).T, a(L0_attn_Wk).T
    wqk = np.concatenate([qT[:, order], kT[:, order]], axis=1)
    parts = [wqk, a(L0_attn_Wv).T, a(L0_attn_Wo).T, a(L0_ffn_sw1), a(L0_ffn_sw3), a(L0_ffn_sw2)]
    parts += [a(L0_ffn_ew1)[e] for e in range(NE)] + [a(L0_ffn_ew2)[e] for e in range(NE)] + [a(L0_ffn_router_w).T]
    wall = np.concatenate([rows_on_partitions(w) for w in parts], axis=1)
    bq, bk = a(L0_attn_bq), a(L0_attn_bk)
    bqk = np.stack([b[order].reshape(2, P)[hf] for b in (bq, bk) for hf in range(2)], axis=1)
    rows = np.concatenate([np.broadcast_to(a(r)[None, :], (P, a(r).shape[0]))
                           for r in (L0_attn_bv, L0_attn_bo, L0_ffn_router_bias)], axis=1)
    inv = (np.float32(1.0) / np.power(np.float32(10000.0), np.arange(0, DH, 2, dtype=np.float32) / np.float32(DH)))
    pos = np.array([NT * p + t for t in range(NT) for p in range(P)], np.float32)
    ang = (pos[None, :] * inv[:, None].astype(np.float32)).astype(np.float64)
    j = np.arange(P) // 8
    sign = np.where(j < DH // 2, 1.0, -1.0)[:, None]
    tabs = np.concatenate([np.cos(ang)[j % 8] / WS, sign * np.sin(ang)[j % 8] / WS], axis=1).astype(np.float32)
    iota = np.broadcast_to(np.arange(NE, dtype=np.float32)[None, :], (P, NE))
    ident = np.eye(P, dtype=np.float32)
    zeros = np.zeros((2, 8 * L), np.float16)
    arrays = dict(x=a(L0_attn_x), wall=wall, bqk=bqk, rows=rows, tabs=tabs, iota=iota, ident=ident, zeros=zeros)
    arrays = {k: np.ascontiguousarray(v) for k, v in arrays.items()}

    nc = bacc.Bacc("TRN2", target_bir_lowering=False, num_devices=1)
    args = [nc.dram_tensor(f"{k}_dram", arrays[k].shape, mb.dt.from_np(arrays[k].dtype), kind="ExternalInput").ap()
            for k in _PARAMS]
    args.append(nc.dram_tensor("out_dram", (NB, L, D), mb.dt.float32, kind="ExternalOutput").ap())
    block_program(nc, *args)
    r = run_bass_kernel_spmd(nc, [{f"{k}_dram": v for k, v in arrays.items()}], core_ids=[0])
    return r.results[0]["out_dram"]
```
